# Optimizing a Trainium2 kernel written in Bass

```python
import numpy as np
import jax
import jax.numpy as jnp

def _softmax(x, axis=-1):
    return jax.nn.softmax(x, axis=axis)

def _gelu(x):
    return jax.nn.gelu(x, approximate=True)

def _silu(x):
    return jax.nn.silu(x)

def _sigmoid(x):
    return jax.nn.sigmoid(x)

def _layernorm(x, axis=-1, eps=1e-05):
    m = jnp.mean(x, axis=axis, keepdims=True)
    v = jnp.var(x, axis=axis, keepdims=True)
    return (x - m) / jnp.sqrt(v + eps)

def _scatter_add(tgt, idx, src, axis=0):
    return tgt.at[idx].add(src)

def _segment_sum(src, seg, n):
    return jax.ops.segment_sum(src, seg, n)
kernel_name = 'mk_decoder_preln_d1_seqx_r4_539bef'

def setup_inputs(seed: int=0):
    np.random.seed(seed)
    _w = jnp.asarray

    def _rec_inputs():
        import jax
        import jax.numpy as jnp
        _rk = jax.random.key(seed)
        x = -0.0002928 + 1 * jax.random.normal(jax.random.fold_in(_rk, 1), (8, 512, 256), jnp.float32)
        _lenS = 512 - jax.random.randint(jax.random.fold_in(_rk, 7), (8,), 0, max(1, 512 // 4) + 1, jnp.int32)
        _lenS2 = 512 - jax.random.randint(jax.random.fold_in(_rk, 8), (8,), 0, max(1, 512 // 4) + 1, jnp.int32)
        _ctx_1024P = jax.random.normal(jax.random.fold_in(_rk, 11), (8, 16, 256), jnp.float32)
        _ctx_1024c = jax.random.dirichlet(jax.random.fold_in(_rk, 511), 0.3 * jnp.ones((16,), jnp.float32), (8, 512))
        _ctx_1024t = jnp.einsum('bsk,bkd->bsd', _ctx_1024c, _ctx_1024P)
        _ctx_1024t = _ctx_1024t * jax.lax.rsqrt(jnp.mean(jnp.square(_ctx_1024t)) + 1e-12) * 0.953939
        ctx_1024 = -1.39393e-06 + 0.999914 * (_ctx_1024t + 0.3 * jax.random.normal(jax.random.fold_in(_rk, 611), (8, 512, 256), jnp.float32))
        _validS = jnp.arange(512)[None, :] < _lenS[:, None]
        _validS2 = jnp.arange(512)[None, :] < _lenS2[:, None]
        _causal = jnp.tril(jnp.ones((512, 512), dtype=bool))
        mask_Bx1xSxS2_ik1 = jnp.where(jnp.broadcast_to(_validS2[:, None, None, :], (8, 1, 512, 512)), 1, 0).astype(jnp.int32)
        return (x, ctx_1024, mask_Bx1xSxS2_ik1)
    x, ctx_1024, mask_Bx1xSxS2_ik1 = _rec_inputs()

    def _L0_attn_setup():
        import jax, jax.numpy as jnp
        import numpy as np
        D_MODEL, D_STATE, EXPAND, D_CONV, HEADDIM = (256, 128, 2, 4, 64)
        D_INNER = EXPAND * D_MODEL
        NHEADS = D_INNER // HEADDIM
        NGROUPS = 1
        CONV_DIM = D_INNER + 2 * NGROUPS * D_STATE
        D_IN_PROJ = 2 * D_INNER + 2 * NGROUPS * D_STATE + NHEADS
        BATCH, SEQ = (2, 1024)
        EPS = 1e-05

        def _mamba2(u, in_proj_w, conv_w, conv_b, dt_bias, A_log, Dp, norm_w, out_proj_w):
            b, l, _ = u.shape
            zxbcdt = u @ in_proj_w.T
            z, xBC, dt = jnp.split(zxbcdt, [D_INNER, D_INNER + CONV_DIM], axis=-1)
            xBC = jnp.transpose(xBC, (0, 2, 1))
            xBC = jax.lax.conv_general_dilated(xBC, conv_w[:, None, :], window_strides=(1,), padding=[(D_CONV - 1, 0)], feature_group_count=CONV_DIM, dimension_numbers=('NCH', 'OIH', 'NCH'))
            xBC = jax.nn.silu(jnp.transpose(xBC, (0, 2, 1)) + conv_b)
            x, Bm, Cm = jnp.split(xBC, [D_INNER, D_INNER + NGROUPS * D_STATE], axis=-1)
            dt = jax.nn.softplus(dt + dt_bias)
            A = -jnp.exp(A_log)
            xh = x.reshape(b, l, NHEADS, HEADDIM)
            dt_t, x_t = (jnp.moveaxis(dt, 1, 0), jnp.moveaxis(xh, 1, 0))
            B_t, C_t = (jnp.moveaxis(Bm, 1, 0), jnp.moveaxis(Cm, 1, 0))

            def step(h, inputs):
                dtk, xk, Bk, Ck = inputs
                decay = jnp.exp(dtk * A)
                h = h * decay[:, :, None, None] + dtk[:, :, None, None] * xk[..., None] * Bk[:, None, None, :]
                y = jnp.einsum('bhpn,bn->bhp', h, Ck)
                return (h, y)
            h0 = jnp.zeros((b, NHEADS, HEADDIM, D_STATE), u.dtype)
            _, ys = jax.lax.scan(step, h0, (dt_t, x_t, B_t, C_t))
            y = jnp.moveaxis(ys, 0, 1) + Dp[None, None, :, None] * xh
            y = y.reshape(b, l, D_INNER)
            y = y * jax.nn.silu(z)
            y = y * jax.lax.rsqrt(jnp.mean(y * y, axis=-1, keepdims=True) + EPS) * norm_w
            return y @ out_proj_w.T
        key = jax.random.key(seed)
        ks = jax.random.split(key, 6)
        sn = lambda k, shape, sc: jax.random.normal(k, shape, jnp.float32) * sc
        dt = jnp.linspace(0.001, 0.1, NHEADS)
        return {'x': sn(ks[0], (BATCH, SEQ, D_MODEL), 1.0), 'ln_w': jnp.ones((D_MODEL,), jnp.float32), 'ln_b': jnp.zeros((D_MODEL,), jnp.float32), 'in_proj_w': sn(ks[1], (D_IN_PROJ, D_MODEL), D_MODEL ** (-0.5)), 'conv_w': sn(ks[2], (CONV_DIM, D_CONV), D_CONV ** (-0.5)), 'conv_b': jnp.zeros((CONV_DIM,), jnp.float32), 'dt_bias': jnp.log(jnp.expm1(dt)).astype(jnp.float32), 'A_log': jnp.log(jnp.arange(1, NHEADS + 1, dtype=jnp.float32)), 'D': jnp.ones((NHEADS,), jnp.float32), 'norm_w': jnp.ones((D_INNER,), jnp.float32), 'out_proj_w': sn(ks[3], (D_MODEL, D_INNER), D_INNER ** (-0.5))}
    _L0_attn_all = _L0_attn_setup()
    _L0_attn_in = {k: v for k, v in _L0_attn_all.items() if k in ('ln_w', 'ln_b', 'in_proj_w', 'conv_w', 'conv_b', 'dt_bias', 'A_log', 'D', 'norm_w', 'out_proj_w')}
    del _L0_attn_all

    def _L0_xattn_setup():
        import jax, jax.numpy as jnp
        import numpy as np
        B, S, E, H = (2, 512, 256, 16)
        D = E // H
        key = jax.random.key(seed)
        ks = jax.random.split(key, 14)
        inp = {'query': jax.random.normal(ks[0], (B, S, E), jnp.float32), 'key': jax.random.normal(ks[1], (B, S, E), jnp.float32), 'value': jax.random.normal(ks[2], (B, S, E), jnp.float32), 'adj': jax.random.normal(ks[3], (S, S), jnp.float32), 'mask': jax.random.randint(ks[4], (B, 1, S, S), 0, 2, jnp.int32)}
        sc = 1.0 / np.sqrt(E)
        inp['Wq'] = jax.random.normal(ks[5], (E, E), jnp.float32) * sc
        inp['bq'] = jax.random.normal(ks[6], (E,), jnp.float32) * sc
        inp['Wk'] = jax.random.normal(ks[7], (E, E), jnp.float32) * sc
        inp['bk'] = jax.random.normal(ks[8], (E,), jnp.float32) * sc
        inp['Wv'] = jax.random.normal(ks[9], (E, E), jnp.float32) * sc
        inp['bv'] = jax.random.normal(ks[10], (E,), jnp.float32) * sc
        inp['Wo'] = jax.random.normal(ks[11], (E, E), jnp.float32) * sc
        inp['bo'] = jax.random.normal(ks[12], (E,), jnp.float32) * sc
        return inp
    _L0_xattn_all = _L0_xattn_setup()
    _L0_xattn_in = {k: v for k, v in _L0_xattn_all.items() if k in ('adj', 'Wq', 'bq', 'Wk', 'bk', 'Wv', 'bv', 'Wo', 'bo')}
    del _L0_xattn_all

    def _L0_ffn_setup():
        import math
        import jax, jax.numpy as jnp
        import numpy as np
        D_CONTENT = 256
        D_POSITION = 32
        NUM_TILES = 8
        BATCH = 8
        SEQ = 512

        def make_pe(seq_len, d_pos):
            pos = jnp.arange(seq_len, dtype=jnp.float32)[:, None]
            div = jnp.exp(jnp.arange(0, d_pos, 2, dtype=jnp.float32) * (-math.log(10000.0) / d_pos))
            ang = pos * div
            pe = jnp.zeros((seq_len, d_pos), dtype=jnp.float32)
            pe = pe.at[:, 0::2].set(jnp.sin(ang))
            pe = pe.at[:, 1::2].set(jnp.cos(ang))
            return pe
        key = jax.random.key(seed)
        k1, k2, k3, k4 = jax.random.split(key, 4)
        x = jax.random.normal(k1, (BATCH, SEQ, D_CONTENT), dtype=jnp.float32)
        tile_sigs = jax.random.normal(k2, (NUM_TILES, D_POSITION), dtype=jnp.float32)
        lim = 1.0 / math.sqrt(D_CONTENT)
        W = jax.random.uniform(k3, (NUM_TILES, D_CONTENT, D_CONTENT), minval=-lim, maxval=lim, dtype=jnp.float32)
        b = jax.random.uniform(k4, (NUM_TILES, D_CONTENT), minval=-lim, maxval=lim, dtype=jnp.float32)
        return {'x': x, 'tile_sigs': tile_sigs, 'W': W, 'b': b}
    _L0_ffn_all = _L0_ffn_setup()
    _L0_ffn_in = {k: v for k, v in _L0_ffn_all.items() if k in ('tile_sigs', 'W', 'b')}
    del _L0_ffn_all
    return {'x': x, 'ctx_1024': ctx_1024, 'mask_Bx1xSxS2_ik1': mask_Bx1xSxS2_ik1, 'L0_attn_ln_w': _L0_attn_in['ln_w'], 'L0_attn_ln_b': _L0_attn_in['ln_b'], 'L0_attn_in_proj_w': _L0_attn_in['in_proj_w'], 'L0_attn_conv_w': _L0_attn_in['conv_w'], 'L0_attn_conv_b': _L0_attn_in['conv_b'], 'L0_attn_dt_bias': _L0_attn_in['dt_bias'], 'L0_attn_A_log': _L0_attn_in['A_log'], 'L0_attn_D': _L0_attn_in['D'], 'L0_attn_norm_w': _L0_attn_in['norm_w'], 'L0_attn_out_proj_w': _L0_attn_in['out_proj_w'], 'L0_xattn_adj': _L0_xattn_in['adj'], 'L0_xattn_Wq': _L0_xattn_in['Wq'], 'L0_xattn_bq': _L0_xattn_in['bq'], 'L0_xattn_Wk': _L0_xattn_in['Wk'], 'L0_xattn_bk': _L0_xattn_in['bk'], 'L0_xattn_Wv': _L0_xattn_in['Wv'], 'L0_xattn_bv': _L0_xattn_in['bv'], 'L0_xattn_Wo': _L0_xattn_in['Wo'], 'L0_xattn_bo': _L0_xattn_in['bo'], 'L0_ffn_tile_sigs': _L0_ffn_in['tile_sigs'], 'L0_ffn_W': _L0_ffn_in['W'], 'L0_ffn_b': _L0_ffn_in['b']}

def reference(x, ctx_1024, mask_Bx1xSxS2_ik1, L0_attn_ln_w, L0_attn_ln_b, L0_attn_in_proj_w, L0_attn_conv_w, L0_attn_conv_b, L0_attn_dt_bias, L0_attn_A_log, L0_attn_D, L0_attn_norm_w, L0_attn_out_proj_w, L0_xattn_adj, L0_xattn_Wq, L0_xattn_bq, L0_xattn_Wk, L0_xattn_bk, L0_xattn_Wv, L0_xattn_bv, L0_xattn_Wo, L0_xattn_bo, L0_ffn_tile_sigs, L0_ffn_W, L0_ffn_b):
    import jax
    import jax.numpy as jnp

    def _L0_attn_ref(x, ln_w, ln_b, in_proj_w, conv_w, conv_b, dt_bias, A_log, D, norm_w, out_proj_w):
        import jax, jax.numpy as jnp
        import numpy as np
        D_MODEL, D_STATE, EXPAND, D_CONV, HEADDIM = (256, 128, 2, 4, 64)
        D_INNER = EXPAND * D_MODEL
        NHEADS = D_INNER // HEADDIM
        NGROUPS = 1
        CONV_DIM = D_INNER + 2 * NGROUPS * D_STATE
        D_IN_PROJ = 2 * D_INNER + 2 * NGROUPS * D_STATE + NHEADS
        BATCH, SEQ = (2, 1024)
        EPS = 1e-05

        def _mamba2(u, in_proj_w, conv_w, conv_b, dt_bias, A_log, Dp, norm_w, out_proj_w):
            b, l, _ = u.shape
            zxbcdt = u @ in_proj_w.T
            z, xBC, dt = jnp.split(zxbcdt, [D_INNER, D_INNER + CONV_DIM], axis=-1)
            xBC = jnp.transpose(xBC, (0, 2, 1))
            xBC = jax.lax.conv_general_dilated(xBC, conv_w[:, None, :], window_strides=(1,), padding=[(D_CONV - 1, 0)], feature_group_count=CONV_DIM, dimension_numbers=('NCH', 'OIH', 'NCH'))
            xBC = jax.nn.silu(jnp.transpose(xBC, (0, 2, 1)) + conv_b)
            x, Bm, Cm = jnp.split(xBC, [D_INNER, D_INNER + NGROUPS * D_STATE], axis=-1)
            dt = jax.nn.softplus(dt + dt_bias)
            A = -jnp.exp(A_log)
            xh = x.reshape(b, l, NHEADS, HEADDIM)
            dt_t, x_t = (jnp.moveaxis(dt, 1, 0), jnp.moveaxis(xh, 1, 0))
            B_t, C_t = (jnp.moveaxis(Bm, 1, 0), jnp.moveaxis(Cm, 1, 0))

            def step(h, inputs):
                dtk, xk, Bk, Ck = inputs
                decay = jnp.exp(dtk * A)
                h = h * decay[:, :, None, None] + dtk[:, :, None, None] * xk[..., None] * Bk[:, None, None, :]
                y = jnp.einsum('bhpn,bn->bhp', h, Ck)
                return (h, y)
            h0 = jnp.zeros((b, NHEADS, HEADDIM, D_STATE), u.dtype)
            _, ys = jax.lax.scan(step, h0, (dt_t, x_t, B_t, C_t))
            y = jnp.moveaxis(ys, 0, 1) + Dp[None, None, :, None] * xh
            y = y.reshape(b, l, D_INNER)
            y = y * jax.nn.silu(z)
            y = y * jax.lax.rsqrt(jnp.mean(y * y, axis=-1, keepdims=True) + EPS) * norm_w
            return y @ out_proj_w.T
        mu = jnp.mean(x, -1, keepdims=True)
        var = jnp.mean((x - mu) ** 2, -1, keepdims=True)
        xn = (x - mu) * jax.lax.rsqrt(var + EPS) * ln_w + ln_b
        return x + _mamba2(xn, in_proj_w, conv_w, conv_b, dt_bias, A_log, D, norm_w, out_proj_w)

    def _L0_xattn_ref(query, key, value, adj, mask, Wq, bq, Wk, bk, Wv, bv, Wo, bo):
        import jax, jax.numpy as jnp
        import numpy as np
        B, S, E, H = (2, 512, 256, 16)
        D = E // H
        b, s, _ = query.shape

        def heads(x, W, bias):
            y = jnp.einsum('bse,ef->bsf', x, W.T) + bias
            return y.reshape(b, s, H, D).transpose(0, 2, 1, 3)
        Q = heads(query, Wq, bq)
        K = heads(key, Wk, bk)
        V = heads(value, Wv, bv)
        scores = jnp.einsum('bhqd,bhkd->bhqk', Q, K) / jnp.sqrt(jnp.float32(D))
        scores = scores + adj[None, None, :, :]
        scores = jnp.where(mask == 0, jnp.float32(-jnp.inf), scores)
        weights = jax.nn.softmax(scores, axis=-1)
        out = jnp.einsum('bhqk,bhkd->bhqd', weights, V)
        out = out.transpose(0, 2, 1, 3).reshape(b, s, E)
        return jnp.einsum('bse,ef->bsf', out, Wo.T) + bo

    def _L0_ffn_ref(x, tile_sigs, W, b):
        import math
        import jax, jax.numpy as jnp
        import numpy as np
        D_CONTENT = 256
        D_POSITION = 32
        NUM_TILES = 8
        BATCH = 8
        SEQ = 512

        def make_pe(seq_len, d_pos):
            pos = jnp.arange(seq_len, dtype=jnp.float32)[:, None]
            div = jnp.exp(jnp.arange(0, d_pos, 2, dtype=jnp.float32) * (-math.log(10000.0) / d_pos))
            ang = pos * div
            pe = jnp.zeros((seq_len, d_pos), dtype=jnp.float32)
            pe = pe.at[:, 0::2].set(jnp.sin(ang))
            pe = pe.at[:, 1::2].set(jnp.cos(ang))
            return pe
        B, S, D = x.shape
        P = tile_sigs.shape[1]
        pe = make_pe(S, P)
        scores = jnp.einsum('sp,tp->st', pe, jnp.sign(tile_sigs))
        idx = jnp.argmax(scores, axis=-1)
        y_all = jnp.einsum('bsd,tod->bsto', x, W) + b
        idx4 = jnp.broadcast_to(idx[None, :, None, None], (B, S, 1, D))
        out = jnp.take_along_axis(y_all, idx4, axis=2)[:, :, 0]
        return out
    x = x + _L0_attn_ref(_layernorm(x, axis=-1), L0_attn_ln_w, L0_attn_ln_b, L0_attn_in_proj_w, L0_attn_conv_w, L0_attn_conv_b, L0_attn_dt_bias, L0_attn_A_log, L0_attn_D, L0_attn_norm_w, L0_attn_out_proj_w)
    x = x + _L0_xattn_ref(_layernorm(x, axis=-1), ctx_1024, ctx_1024, L0_xattn_adj, mask_Bx1xSxS2_ik1, L0_xattn_Wq, L0_xattn_bq, L0_xattn_Wk, L0_xattn_bk, L0_xattn_Wv, L0_xattn_bv, L0_xattn_Wo, L0_xattn_bo)
    x = x + _L0_ffn_ref(_layernorm(x, axis=-1), L0_ffn_tile_sigs, L0_ffn_W, L0_ffn_b)
    return x

_drawn_inputs = setup_inputs


def setup_inputs(seed=0):
    import zlib

    import numpy as np

    out = dict(_drawn_inputs(seed))
    spreads = {'L0_attn_ln_w': (1.0, 0.2),
     'L0_attn_ln_b': (0.0, 0.1),
     'L0_attn_conv_b': (0.0, 0.1),
     'L0_attn_D': (1.0, 0.6),
     'L0_attn_norm_w': (1.0, 0.2)}
    factors = {'L0_xattn_bq': 8.0, 'L0_xattn_bk': 8.0, 'L0_ffn_b': 3.753}
    for name, (base, spread) in spreads.items():
        noise = np.random.default_rng([zlib.crc32(name.encode()), seed]).standard_normal(out[name].shape)
        drawn = base * np.exp(spread * noise) if base else spread * noise
        out[name] = jnp.asarray(drawn.astype(out[name].dtype))
    for name, factor in factors.items():
        out[name] = (out[name] * factor).astype(out[name].dtype)
    return out
```

```python
from contextlib import ExitStack

import numpy as np

import concourse.bass as bass
from concourse import mybir

F32 = mybir.dt.float32
F32R = mybir.dt.float32r
I32 = mybir.dt.int32
U32 = mybir.dt.uint32
ALU = mybir.AluOpType
ACT = mybir.ActivationFunctionType
AX = mybir.AxisListType

P = 128
B, S, E = 8, 512, 256
C = S // P
KE = E // P
DI, DS, NH, HD, DC = 512, 128, 8, 64, 4
KI = DI // P
CT = (DI + 2 * DS) // P
AH, AD = 16, 16
HG = 4
G = AH // HG
VW = 32
UG = HG * C
UNITS = G * UG
HS = 2
PRE = 3
DRAIN = 8
SLOTS = UNITS + DRAIN
NT = 8
PD = 32
EPS = 1e-5
MASKED = -1e30
SEG = 32
SEGS = S // SEG + NT
BLOCKS = SEGS * SEG // P
PAIRS = BLOCKS * B // 2
BUFS = 3
ROW = B * E
RT = dict(slot=P, first=NT, seg_at=S // SEG, seg=SEGS, before=NT * NT, block_at=BLOCKS - 1, blk=BLOCKS, blk_slot=BLOCKS, pos1=C)


CONV_ORDER = (4, 5, 0, 1, 2, 3)
ON_POOL, ON_DVE = (4, 0, 2, 3), (5, 1)
HEAD = ("ln1", "ln2", "lnT", "dt1", "dt2", "bc", "conv", "cum")


def schedule():
    when = {e: [[] for _ in range(SLOTS)] for e in ("sp", "pe", "act", "dve", "pool")}

    def put(stage, slot, **shift):
        for e in when:
            when[e][slot + shift.get(e, 0)].append(stage)

    put(("k",), 0, dve=1, sp=2)
    for i, mt in enumerate(CONV_ORDER):
        put(("silu", mt), i, dve=1)
    put(("v",), 3, dve=1, sp=2)
    for c in range(C):
        put(("am", c), 8 + 2 * c)
    for c in range(C):
        t = 6 + 11 * c
        put(("seg", c), t + 1, pool=-1)
        put(("gx", c), t + 1, dve=1, pool=1)
        put(("z", c), t + 2, act=1, dve=2)
        put(("w", c), t + 3)
        put(("y", c), t + 4, dve=1)
        put(("gate", c), t + 6)
        put(("gate2", c), t + 7)
        put(("o", c), t + 7)
        put(("x1", c), t + 8, dve=1, pool=1)
        put(("xq", c), t + 10)
    put(("q1",), 50)
    put(("q2",), 51, dve=1, sp=2)
    put(("ln1",), 46)
    put(("ln2",), 53)
    put(("lnT",), 54, sp=1)
    put(("dt1",), 55, dve=1, act=2)
    for i, mt in enumerate(CONV_ORDER):
        put(("bc", mt), (55, 57, 58, 60, 61, 63)[i])
        put(("conv", mt), (56, 58, 59, 61, 62, 64)[i])
    for i in range(4):
        put(("dt2", i), 59 + i)
    put(("cum",), 64)
    return when


WHEN = schedule()
M_TILES = []
for _head in (True, False):
    for _slot in WHEN["pe"]:
        for _s in _slot:
            if (_s[0] in HEAD) != _head:
                continue
            M_TILES += {
                "lnT": [("lnT", 0), ("lnT", 1)], "dt1": [("dt",)], "bc": [_s], "cum": [("cum",)], "z": [_s],
                "k": [("k", 0), ("k", 1)], "v": [("v", 0), ("v", 1)], "q1": [("xqT", 0), ("xqT", 1)],
                "q2": [("q", 0), ("q", 1)],
                "seg": [("seg", 0) + _s[1:], ("seg", 1) + _s[1:]], "gx": [("gb",) + _s[1:], ("xt",) + _s[1:]],
                "y": [("inter",) + _s[1:]] * (_s[-1] != 0) + [("intra",) + _s[1:]] + [("state",) + _s[1:]] * (_s[-1] != C - 1),
                "o": [("yT",) + _s[1:]], "x1": [("out",) + _s[1:]],
            }.get(_s[0], [])
M_BANKS = 3


def build(nc, t):
    ctx = ExitStack()
    with ctx:
        def sb(name, shape, dt=F32):
            return ctx.enter_context(nc.sbuf_tensor(name, shape, dt))

        def sem(name):
            return ctx.enter_context(nc.semaphore(name))

        qk_d = nc.dram_tensor("qk_d", (B, 2, 2, E, S), F32, kind="Internal").ap()
        x2_d = nc.dram_tensor("x2_d", (S, ROW), F32, kind="Internal").ap()

        ident = sb("ident", [P, P])
        triu = sb("triu", [P, P])
        stril = sb("stril", [P, P])
        ones = sb("ones", [P, P])
        nhalf = sb("nhalf", [P, 8])
        wxbc = sb("wxbc", [P, KE, CT * P])
        wz = sb("wz", [P, KE, DI])
        wdt = sb("wdt", [P, KE, NH])
        wout = sb("wout", [P, KI, E])
        wq, wk, wv, wo = (sb(n, [P, KE, E]) for n in ("wq", "wk", "wv", "wo"))
        lnw, lnb = sb("lnw", [P, KE]), sb("lnb", [P, KE])
        cw, cb = sb("cw", [P, CT, DC]), sb("cb", [P, CT])
        dtb, nega = sb("dtb", [P, C, NH]), sb("nega", [P, NH])
        alog = sb("alog", [P, NH])
        dsk = sb("dsk", [P, NH])
        nw = sb("nw", [P, KI])
        bq, bk = sb("bq", [P, KE]), sb("bk", [P, KE])
        bvb, bob = sb("bvb", [P, E]), sb("bob", [P, E])

        x_in = sb("x_in", [P, C, E])
        ctx_in = sb("ctx_in", [P, KE, S])
        st, mv, ve, rs = sb("st", [P, C, 6]), sb("mv", [P, C, 2]), sb("ve", [P, C, 2]), sb("rs", [P, C, 2])
        xn, xr = sb("xn", [P, C, E]), sb("xr", [P, C, E])
        x1, xq = sb("x1", [P, C, E]), xn
        xnT = sb("xnT", [P, KE, S])
        pre = sb("pre", [P, PRE, DC - 1 + S])
        xc = sb("xc", [P, CT, S])
        th = sb("th", [P, 2, S])
        zt, zs = sb("zt", [P, 2, DI]), sb("zs", [P, DI])
        dts = sb("dts", [P, 8, C, NH])
        dt, dA = sb("dt", [P, C, NH]), sb("dA", [P, C, NH])
        ecum = sb("ecum", [P, 2, C, NH])
        L = sb("L", [P, NH, P])
        dmask = L
        Gm, Bt = sb("Gm", [P, P]), sb("Bt", [P, DS])
        xt, xdt, xw = (sb(n, [P, NH, HD]) for n in ("xt", "xdt", "xw"))
        xD = xt
        ti, yg = sb("ti", [P, NH, HD]), sb("yg", [P, NH, HD])
        ygT = sb("ygT", [P, KI, P])
        tap = ygT
        state = sb("state", [P, NH, HD])
        sdec = state
        ss, se, rr = sb("ss", [P, 1]), sb("se", [P, 1]), sb("rr", [P, 1])
        st2, mv2, ve2, r2 = sb("st2", [P, 6]), sb("mv2", [P, 2]), sb("ve2", [P, 1]), sb("r2", [P, 1])
        x1b, xqT, kf = x1, xnT, zt
        kp = sb("kp", [P, 2, KE, S], F32R)
        qf, qp_ = kf, kp
        vm = sb("vm", [P, C, AH, VW])
        am_m = sb("am_m", [P, C, S])

        q_st = sb("q_st", [P, 2, HS, S], F32R)
        k_st = sb("k_st", [P, 2, HS, S], F32R)
        va = sb("va", [P, C, AH, VW])
        am = sb("am", [P, C, S])
        x1a = sb("x1a", [P, C, E])
        T = sb("T", [P, 2, S])
        nmx = sb("nmx", [P, 2])
        Pr = sb("Pr", [P, 2, S])
        PT = sb("PT", [P, HG, C, S])
        OTs = sb("OTs", [P, S])
        rden = sb("rden", [P, C, HG])
        On = sb("On", [P, C, AH, AD])
        OnT = OTs[:, :].rearrange("p (b k i) -> p b k i", b=2, k=KE)

        rt = sb("rt", [P, sum(RT.values())])
        row_of, expert_of = sb("row_of", [P, BLOCKS], I32), sb("expert_of", [P, BLOCKS], I32)
        seg_expert = sb("seg_expert", [1, SEGS], I32)
        flat = PT[:, :, :, :].rearrange("p h k s -> p (h k s)")
        w_f = flat[:, 0:KE * NT * E].rearrange("p (k t e) -> p k t e", k=KE, t=NT)
        x_f = [flat[:, KE * NT * E:KE * NT * E + ROW], flat[:, KE * NT * E + ROW:KE * NT * E + 2 * ROW],
               xc[:, :, :].rearrange("p c s -> p (c s)")[:, 0:ROW]]
        seg_w = [ap[:, :, :].rearrange("p c s -> p (c s)").rearrange("p (j k e) -> p j k e", j=P // SEG, k=KE) for ap in (am_m, am)]
        b_f = vm[:, :, :, :].rearrange("p c h v -> p (c h v)")[:, 0:BLOCKS * E].rearrange("p (k e) -> p k e", e=E)
        n_f, t_f = zt, xnT
        small = ti[:, :, :].rearrange("p h d -> p (h d)").rearrange("p (b n) -> p b n", b=2)
        st_f, mv_f = small[:, :, 0:6 * B], small[:, :, 6 * B:8 * B]
        ve_f, r_f = small[:, :, 8 * B:9 * B], small[:, :, 9 * B:10 * B]

        pm = [ctx.enter_context(nc.psum_tensor(f"pm{i}", [P, 512], F32)) for i in range(M_BANKS)]
        ps = [ctx.enter_context(nc.psum_tensor(f"ps{i}", [P, 512], F32)) for i in range(2)]
        pt = [ctx.enter_context(nc.psum_tensor(f"pt{i}", [P, 512], F32)) for i in range(2)]
        po = ctx.enter_context(nc.psum_tensor("po", [P, 512], F32))

        consts = sem("consts")
        bank_fills = [sum(1 for i in range(len(M_TILES)) if i % M_BANKS == k) for k in range(M_BANKS)]
        m_full = [sem(f"m_full{k}") for k in range(M_BANKS)]
        m_read = [sem(f"m_read{k}") for k in range(M_BANKS)]
        setup = {n: sem(f"setup_{n}") for n in ("act", "dve", "ready")}
        PER = dict(
            x_loaded=16, ctx_loaded=16, mask_loaded=16, stats=C, mean_var=C, var_eps=2, rstd=1, normed=C, ln_x=C, residual=1,
            conv_pool=4 * DC, tap_product=4 * (DC - 1), conv_dve=2 * DC, tanh=CT, silu=CT, z_tanh=C, dt_step=12, dt_exp=1, dt_series=2, dt_ready=2, gram_masked=C, decay_mask=C, L=2 * C,
            weights=C, x_dt=C, x_decayed=C - 1, x_D=C, y_inter=C - 1, y_gated=C, sumsq=C, meansq=C, gate_rstd=C, state_decayed=C - 2,
            stats2=C, mean_var2=C, var_eps2=C, rstd2=C, query_normed=C, x1_bias=C, k_high=2, k_low=2, q_high=2, q_low=2,
            v_half=2, mask_bias=C, score_bias=16, qk_out=16 * 8,
            va_moved=16, x1a_moved=16, bias_moved01=16, bias_moved23=16,
            st_in0=16 * 8 * 4, st_in1=16 * 8 * 4, score=UNITS, row_max=UNITS, probs=UNITS, turned=UNITS, evac_act=UNITS // 2, evac_dve=UNITS // 2,
            pv=G, sums_out=G, sums_turned=G, recip=G, heads_normed=G, heads_turned=C, heads_copied=C, projected=C, x2_rows=C,
            x2_out0=16 * 2, x2_out1=16 * 2)
        sems = {n: sem(n) for n in PER}

        def at(name, b, k):
            v = b * PER[name] + k
            return max(v, 0) if isinstance(v, int) else v

        def alone(eng, sem, v):
            if not isinstance(v, int):
                v = eng.to_reg(v)
                eng.wait_ge(consts, CONSTS)
            return sem, v

        def tile(name):
            i = M_TILES.index(name)
            return i % M_BANKS, i // M_BANKS + 1

        def bank(name):
            return pm[tile(name)[0]]

        def full(name):
            return m_full[tile(name)[0]]

        def read(name):
            return m_read[tile(name)[0]]

        def full_at(name, b):
            v = b * bank_fills[tile(name)[0]] + tile(name)[1]
            return max(v, 0) if isinstance(v, int) else v

        def read_at(name, b):
            return full_at(name, b)

        def free_at(name, b):
            return b * bank_fills[tile(name)[0]] + tile(name)[1] - 1

        step = {n: sem(n) for n in (
            "f_signs", "f_scores", "f_routed", "f_counts", "f_onehot", "f_slots", "f_tables", "f_rows", "f_w", "f_placed", "f_b",
            "f_stats", "f_mean_var", "f_var_eps", "f_rstd", "f_normed", "f_turned", "f_copied", "f_product", "f_sum", "f_biased")}
        f_in = [sem(f"f_in{i}") for i in range(BUFS)]
        f_out = [sem(f"f_out{i}") for i in range(BUFS)]
        route_loads = sem("route_loads")
        rcol, _n = {}, 0
        for _k, _w in RT.items():
            rcol[_k] = rt[:, _n:_n + _w]
            _n += _w
        tmp = PT[:, :, :, :].rearrange("p h k s -> p (h k s)")
        pos_e, sig_e = tmp[0:PD, 0:S], tmp[0:PD, S:S + NT]
        LEFT, RIGHT, OH, ST = 1024, 2048, 2600, 2700

        loads = [
            (ident[:, :], t["ident"]), (triu[:, :], t["triu"]), (stril[:, :], t["stril"]),
            (wxbc[:, :, :], t["wxbc"].rearrange("(k p) n -> p k n", p=P)),
            (wz[:, :, :], t["wz"].rearrange("(k p) n -> p k n", p=P)),
            (wdt[:, :, :], t["wdt"].rearrange("(k p) n -> p k n", p=P)),
            (wout[:, :, :], t["wout"].rearrange("(k p) n -> p k n", p=P)),
            (wq[:, :, :], t["wq"].rearrange("(k p) n -> p k n", p=P)),
            (wk[:, :, :], t["wk"].rearrange("(k p) n -> p k n", p=P)),
            (wv[:, :, :], t["wv"].rearrange("(k p) n -> p k n", p=P)),
            (wo[:, :, :], t["wo"].rearrange("(k p) n -> p k n", p=P)),
            (lnw[:, :], t["ln_w"].rearrange("(k p) -> p k", p=P)), (lnb[:, :], t["ln_b"].rearrange("(k p) -> p k", p=P)),
            (cw[:, :, :], t["conv_w"].rearrange("(k p) j -> p k j", p=P)), (cb[:, :], t["conv_b"].rearrange("(k p) -> p k", p=P)),
            (alog[:, :], t["A_log"].partition_broadcast(P)), (dsk[:, :], t["D"].partition_broadcast(P)),
            (nw[:, :], t["norm_w"].rearrange("(k p) -> p k", p=P)),
            (bq[:, :], t["bq"].rearrange("(k p) -> p k", p=P)), (bk[:, :], t["bk"].rearrange("(k p) -> p k", p=P)),
            (bvb[:, :], t["bv"].partition_broadcast(P)), (bob[:, :], t["bo"].partition_broadcast(P)),
        ] + [(dtb[:, c, :], t["dt_bias"].partition_broadcast(P)) for c in range(C)]
        CONSTS = 16 * len(loads)

        def batches(eng, body, peeled=0):
            body(None, None, 0)
            body(0, None, 1)
            body(1, 0, 2)
            with eng.Fori(1, B - 2 - peeled) as a:
                body(a + 1, a, a + 2)
            for a in range(B - 2 - peeled, B - 2):
                body(a + 1, a, a + 2)
            body(B - 1, B - 2, None)
            body(None, B - 1, None)

        def unit(u):
            w = u % UG
            return u // UG, w % C, w // C

        def evac_by(u):
            return "evac_dve" if u % 2 else "evac_act"

        def mt_order(mt):
            return CONV_ORDER.index(mt)

        def conv_by(mt):
            return "conv_pool" if mt in ON_POOL else "conv_dve"

        def taps_at(mt, taps):
            return DC * (ON_POOL if mt in ON_POOL else ON_DVE).index(mt) + taps

        with nc.allow_non_contiguous_dma("vectors of weights, once"), nc.Block() as block:

            @block.sync
            def _(sp):
                sp.dma_start(pos_e, t["pe"]).then_inc(route_loads, 16)
                sp.dma_start(sig_e, t["sigs"]).then_inc(route_loads, 16)
                sp.dma_start(rt[:, :], t["rt"]).then_inc(route_loads, 16)
                for dst, src in loads:
                    sp.dma_start(dst, src).then_inc(consts, 16)

                def load_x(b):
                    sp.dma_start(x_in[:, :, :], t["x"][bass.ds(b * S, S), :].rearrange("(c p) e -> p c e", p=P)).then_inc(sems["x_loaded"], 16)

                def load_ctx(b):
                    sp.dma_start(ctx_in[:, :, :], t["ctxT"][bass.ds(b * E, E), :].rearrange("(k p) s -> p k s", p=P)).then_inc(sems["ctx_loaded"], 16)

                def load_mask(b):
                    sp.dma_start(am_m[:, :, :].bitcast(I32), t["mask"][bass.ds(b * S, S), :].rearrange("(c p) s -> p c s", p=P)).then_inc(sems["mask_loaded"], 16)

                def out_parts(b, which, parts):
                    for hl in range(2):
                        for k in range(KE):
                            sp.dma_start(qk_d[bass.ds(b, 1), which, hl, k * P:(k + 1) * P, :].rearrange("o p s -> p (o s)"),
                                         parts[:, hl, k, :].bitcast(F32)).then_inc(sems["qk_out"], 16)

                def stage(a, n):
                    for which, st_, order in ((0, q_st, (0, 0, 1, 1)), (1, k_st, (0, 1, 0, 1))):
                        for r, hl in enumerate(order):
                            src = qk_d[bass.ds(a, 1), which, hl, n * HS * AD:(n + 1) * HS * AD, :]
                            sp.dma_start(st_[r * AD:(r + 1) * AD, n % 2, :, :].bitcast(F32),
                                         src.rearrange("o (h d) s -> d (o h) s", d=AD)).then_inc(sems[f"st_in{n % 2}"], 16)

                load_x(0), load_ctx(0), load_mask(0)

                def body(b, a, nxt):
                    for u in range(SLOTS):
                        if b is not None and u == 0 and not (isinstance(b, int) and b == 0):
                            sp.wait_ge(*alone(sp, sems["bias_moved01"], at("bias_moved01", b, 0)))
                            sp.wait_ge(*alone(sp, sems["bias_moved23"], at("bias_moved23", b, 0)))
                            load_mask(b)
                        if a is not None:
                            if u and u % (HS * C) == 0 and u // (HS * C) + 1 < AH // HS:
                                n = u // (HS * C) + 1
                                sp.wait_ge(*alone(sp, sems["score"], at("score", a, HS * C * (n - 1))))
                                stage(a, n)
                            if u >= UNITS + 3 and u - UNITS - 3 < C:
                                q = u - UNITS - 3
                                sp.wait_ge(*alone(sp, sems["x2_rows"], at("x2_rows", a, q + 1)))
                                sp.dma_start(x2_d[q * P:(q + 1) * P, bass.ds(a * E, E)], x1a[:, q, :]).then_inc(sems[f"x2_out{q % 2}"], 16)
                        for stg in WHEN["sp"][u]:
                            if stg == ("lnT",) and nxt is not None and not (isinstance(nxt, int) and nxt == B - 1):
                                sp.wait_ge(*alone(sp, sems["normed"], at("normed", nxt, C)))
                                sp.wait_ge(*alone(sp, sems["residual"], at("residual", nxt, 1)))
                                load_x(nxt + 1)
                            if stg == ("k",) and b is not None:
                                sp.wait_ge(*alone(sp, sems["k_low"], at("k_low", b, 2)))
                                sp.wait_ge(*alone(sp, sems["k_high"], at("k_high", b, 2)))
                                out_parts(b, 1, kp)
                            if stg == ("v",) and nxt is not None and b is not None:
                                sp.wait_ge(*alone(sp, full(("v", 1)), full_at(("v", 1), b)))
                                load_ctx(b + 1)
                            if stg == ("q2",) and b is not None:
                                sp.wait_ge(*alone(sp, sems["q_low"], at("q_low", b, 2)))
                                sp.wait_ge(*alone(sp, sems["q_high"], at("q_high", b, 2)))
                                out_parts(b, 0, kp)
                        if b is not None:
                            if u == UNITS - HS * C + 1:
                                sp.wait_ge(*alone(sp, sems["qk_out"], at("qk_out", b, 16 * 8)))
                                sp.wait_ge(*alone(sp, sems["score"], at("score", b, -HS * C)))
                                stage(b, 0)
                            if u == UNITS:
                                sp.wait_ge(*alone(sp, sems["score_bias"], at("score_bias", b, 16)))
                                sp.wait_ge(*alone(sp, sems["row_max"], at("row_max", b, 0)))
                                sp.dma_start(am[:, 0:2, :], am_m[:, 0:2, :]).then_inc(sems["bias_moved01"], 16)
                                sp.dma_start(am[:, 2:4, :], am_m[:, 2:4, :]).then_inc(sems["bias_moved23"], 16)
                                sp.wait_ge(*alone(sp, sems["score"], at("score", b, 0)))
                                stage(b, 1)
                            if u == UNITS + 3:
                                sp.wait_ge(*alone(sp, sems["v_half"], at("v_half", b, 2)))
                                sp.wait_ge(*alone(sp, read(("v", 0)), read_at(("v", 0), b)))
                                sp.wait_ge(*alone(sp, read(("v", 1)), read_at(("v", 1), b)))
                                sp.wait_ge(*alone(sp, sems["pv"], at("pv", b, 0)))
                                sp.dma_start(va[:, :, :, :], vm[:, :, :, :]).then_inc(sems["va_moved"], 16)
                            if u == SLOTS - 1:
                                sp.wait_ge(*alone(sp, sems["x1_bias"], at("x1_bias", b, C)))
                                sp.wait_ge(*alone(sp, sems["x2_out0"], at("x2_out0", b, 0)))
                                sp.wait_ge(*alone(sp, sems["x2_out1"], at("x2_out1", b, 0)))
                                sp.dma_start(x1a[:, :, :], x1b[:, :, :]).then_inc(sems["x1a_moved"], 16)

                batches(sp, body, peeled=1)
                sp.wait_ge(sems["pv"], at("pv", B, 0))
                sp.dma_start(w_f, t["w_f"].rearrange("(k p) t e -> p k t e", p=P)).then_inc(step["f_w"], 16)
                for i in range(BUFS):
                    sp.wait_ge(f_out[i], 16 * (BLOCKS // BUFS))

            @block.tensor
            def _(pe):
                pe.wait_ge(step["f_signs"], 1)
                for c in range(C):
                    ins = pe.matmul(po[:, c * NT:(c + 1) * NT], pos_e[:, c * P:(c + 1) * P], sig_e, start=True, stop=True)
                ins.then_inc(step["f_scores"], 1)
                pe.wait_ge(consts, CONSTS)
                pe.wait_ge(setup["ready"], 3)
                pe.wait_ge(step["f_onehot"], 1)
                oh = tmp[:, OH:OH + C * NT]
                for c in range(C):
                    for k in range(c + 1):
                        pe.matmul(po[:, c * NT:(c + 1) * NT], triu[:, :] if k == c else ones[:, :], oh[:, k * NT:(k + 1) * NT], start=(k == 0), stop=(k == c))
                for c in range(C):
                    ins = pe.matmul(po[:, C * NT:(C + 1) * NT], ones[:, :], oh[:, c * NT:(c + 1) * NT], start=(c == 0), stop=(c == C - 1))
                ins.then_inc(step["f_counts"], 1)
                pe.wait_ge(step["f_tables"], 1)
                for c in range(C):
                    ins = pe.matmul(po[:, 0:BLOCKS], tmp[:, LEFT + c * P:LEFT + (c + 1) * P], tmp[:, RIGHT + c * BLOCKS:RIGHT + (c + 1) * BLOCKS],
                                    start=(c == 0), stop=(c == C - 1))
                ins.then_inc(step["f_slots"], 1)

                def mm(out, lhsT, rhs, first, last):
                    return pe.matmul(out, lhsT, rhs, start=first, stop=last)

                def m(stg, b):
                    k = stg[0]
                    if k == "lnT":
                        pe.wait_ge(sems["normed"], at("normed", b, C))
                        for kt in range(KE):
                            pe.wait_ge(read(("lnT", kt)), free_at(("lnT", kt), b))
                            for c in range(C):
                                ins = pe.transpose(bank(("lnT", kt))[:, c * P:(c + 1) * P], xn[:, c, kt * P:(kt + 1) * P], ident[:, :])
                            ins.then_inc(full(("lnT", kt)), 1)
                    if k == "dt1":
                        pe.wait_ge(read(("dt",)), free_at(("dt",), b))
                        for kt in range(KE):
                            pe.wait_ge(read(("lnT", kt)), read_at(("lnT", kt), b))
                        for c in range(C):
                            for kt in range(KE):
                                ins = mm(bank(("dt",))[:, c * NH:(c + 1) * NH], xnT[:, kt, c * P:(c + 1) * P], wdt[:, kt, :], kt == 0, kt == KE - 1)
                        ins.then_inc(full(("dt",)), 1)
                    if k == "bc":
                        pe.wait_ge(read(stg), free_at(stg, b))
                        for kt in range(KE):
                            ins = mm(bank(stg)[:, :], wxbc[:, kt, stg[1] * P:(stg[1] + 1) * P], xnT[:, kt, :], kt == 0, kt == KE - 1)
                        ins.then_inc(full(stg), 1)
                    if k == "z":
                        pe.wait_ge(read(stg), free_at(stg, b))
                        for kt in range(KE):
                            ins = mm(bank(stg)[:, :], xnT[:, kt, stg[1] * P:(stg[1] + 1) * P], wz[:, kt, :], kt == 0, kt == KE - 1)
                        ins.then_inc(full(stg), 1)
                    if k == "cum":
                        pe.wait_ge(read(("cum",)), free_at(("cum",), b))
                        pe.wait_ge(sems["dt_ready"], at("dt_ready", b, 2))
                        mm(bank(("cum",))[:, 0:C * NH], triu[:, :], dA[:, :, :].rearrange("p c h -> p (c h)"), True, True)
                        mm(bank(("cum",))[:, C * NH:2 * C * NH], ones[:, :], dA[:, :, :].rearrange("p c h -> p (c h)"), True, True).then_inc(full(("cum",)), 1)
                    if k == "k":
                        pe.wait_ge(sems["ctx_loaded"], at("ctx_loaded", b, 16))
                        for ct in range(KE):
                            pe.wait_ge(read(("k", ct)), free_at(("k", ct), b))
                            for kt in range(KE):
                                ins = mm(bank(("k", ct))[:, :], wk[:, kt, ct * P:(ct + 1) * P], ctx_in[:, kt, :], kt == 0, kt == KE - 1)
                            ins.then_inc(full(("k", ct)), 1)
                    if k == "v":
                        for j in range(2):
                            pe.wait_ge(read(("v", j)), free_at(("v", j), b))
                            for c in (2 * j, 2 * j + 1):
                                for kt in range(KE):
                                    ins = mm(bank(("v", j))[:, (c % 2) * E:(c % 2 + 1) * E], ctx_in[:, kt, c * P:(c + 1) * P], wv[:, kt, :], kt == 0, kt == KE - 1)
                            ins.then_inc(full(("v", j)), 1)
                    if k == "seg":
                        c = stg[1]
                        pe.wait_ge(sems["decay_mask"], at("decay_mask", b, c + 1))
                        for j in range(2):
                            pe.wait_ge(read(("seg", j, c)), free_at(("seg", j, c), b))
                            mm(bank(("seg", j, c))[:, :], stril[:, :], dmask[:, 4 * j:4 * j + 4, :].rearrange("p h i -> p (h i)"), True, True).then_inc(full(("seg", j, c)), 1)
                    if k == "gx":
                        c = stg[1]
                        cs = slice(c * P, (c + 1) * P)
                        pe.wait_ge(sems["silu"], at("silu", b, CT))
                        pe.wait_ge(read(("gb", c)), free_at(("gb", c), b))
                        mm(bank(("gb", c))[:, 0:P], xc[:, 4, cs], xc[:, 5, cs], True, True)
                        pe.transpose(bank(("gb", c))[:, P:2 * P], xc[:, 4, cs], ident[:, :]).then_inc(full(("gb", c)), 1)
                        pe.wait_ge(read(("xt", c)), free_at(("xt", c), b))
                        for kt in range(KI):
                            ins = pe.transpose(bank(("xt", c))[:, kt * P:(kt + 1) * P], xc[:, kt, cs], ident[:, :])
                        ins.then_inc(full(("xt", c)), 1)
                    if k == "y":
                        c = stg[1]
                        if c:
                            pe.wait_ge(read(("inter", c)), free_at(("inter", c), b))
                            pe.wait_ge(read(("state", c - 1)), read_at(("state", c - 1), b))
                            mm(bank(("inter", c))[:, :], xc[:, 5, c * P:(c + 1) * P], state[:, :, :].rearrange("p h d -> p (h d)"), True, True).then_inc(full(("inter", c)), 1)
                        pe.wait_ge(read(("intra", c)), free_at(("intra", c), b))
                        pe.wait_ge(sems["weights"], at("weights", b, c + 1))
                        pe.wait_ge(sems["x_dt"], at("x_dt", b, c + 1))
                        for h in range(NH):
                            ins = mm(bank(("intra", c))[:, h * HD:(h + 1) * HD], L[:, h, :], xdt[:, h, :], True, True)
                        ins.then_inc(full(("intra", c)), 1)
                        if c < C - 1:
                            pe.wait_ge(read(("state", c)), free_at(("state", c), b))
                            pe.wait_ge(sems["x_decayed"], at("x_decayed", b, c + 1))
                            mm(bank(("state", c))[:, :], Bt[:, :], xw[:, :, :].rearrange("p h d -> p (h d)"), True, True).then_inc(full(("state", c)), 1)
                    if k == "o":
                        c = stg[1]
                        pe.wait_ge(read(("yT", c)), free_at(("yT", c), b))
                        pe.wait_ge(sems["y_gated"], at("y_gated", b, c + 1))
                        for kt in range(KI):
                            ins = pe.transpose(bank(("yT", c))[:, kt * P:(kt + 1) * P], yg[:, :, :].rearrange("p h d -> p (h d)")[:, kt * P:(kt + 1) * P], ident[:, :])
                        ins.then_inc(full(("yT", c)), 1)
                    if k == "x1":
                        c = stg[1]
                        pe.wait_ge(read(("out", c)), free_at(("out", c), b))
                        pe.wait_ge(read(("yT", c)), read_at(("yT", c), b))
                        for kt in range(KI):
                            ins = mm(bank(("out", c))[:, 0:E], ygT[:, kt, :], wout[:, kt, :], kt == 0, kt == KI - 1)
                        ins.then_inc(full(("out", c)), 1)
                    if k == "q1":
                        pe.wait_ge(sems["query_normed"], at("query_normed", b, C))
                        for kt in range(KE):
                            pe.wait_ge(read(("xqT", kt)), free_at(("xqT", kt), b))
                            for c in range(C):
                                ins = pe.transpose(bank(("xqT", kt))[:, c * P:(c + 1) * P], xq[:, c, kt * P:(kt + 1) * P], ident[:, :])
                            ins.then_inc(full(("xqT", kt)), 1)
                    if k == "q2":
                        for kt in range(KE):
                            pe.wait_ge(read(("xqT", kt)), read_at(("xqT", kt), b))
                        for ct in range(KE):
                            pe.wait_ge(read(("q", ct)), free_at(("q", ct), b))
                            for kt in range(KE):
                                ins = mm(bank(("q", ct))[:, :], wq[:, kt, ct * P:(ct + 1) * P], xqT[:, kt, :], kt == 0, kt == KE - 1)
                            ins.then_inc(full(("q", ct)), 1)

                def score(a, u):
                    g, qt, hh = unit(u)
                    n, hs = u // (HS * C), u // C % HS
                    if u % (HS * C) == 0:
                        pe.wait_ge(sems[f"st_in{n % 2}"], at(f"st_in{n % 2}", a, 16 * 8 * (n // 2 + 1)))
                    pe.wait_ge(sems["row_max"], at("row_max", a, u - 1))
                    mm(ps[u % 2][:, :], q_st[:, n % 2, hs, qt * P:(qt + 1) * P], k_st[:, n % 2, hs, :], True, True).then_inc(sems["score"], 1)

                def turn(a, u):
                    pe.wait_ge(sems["probs"], at("probs", a, u + 1))
                    if u < 2:
                        pe.wait_ge(sems["x2_rows"], at("x2_rows", a, 0))
                    pe.wait_ge(sems[evac_by(u - 2)], at(evac_by(u - 2), a, (u - 2) // 2 + 1))
                    for kt in range(C):
                        ins = pe.transpose(pt[u % 2][:, kt * P:(kt + 1) * P], Pr[:, u % 2, kt * P:(kt + 1) * P], ident[:, :])
                    ins.then_inc(sems["turned"], 1)

                def pv(a, g):
                    if g == 0:
                        pe.wait_ge(sems["va_moved"], at("va_moved", a, 16))
                    pe.wait_ge(sems[evac_by(UG * g + UG - 2)], at(evac_by(UG * g + UG - 2), a, (UG * g + UG - 2) // 2 + 1))
                    pe.wait_ge(sems[evac_by(UG * g + UG - 1)], at(evac_by(UG * g + UG - 1), a, (UG * g + UG - 1) // 2 + 1))
                    pe.wait_ge(sems["heads_normed"], at("heads_normed", a, g))
                    for kt in range(C):
                        for hh in range(HG):
                            ins = pe.matmul(po[VW * hh:VW * (hh + 1), :], va[:, kt, g * HG + hh, :], PT[:, hh, kt, :],
                                            start=(kt == 0), stop=(kt == C - 1), tile_position=(0, VW * hh), skip_group_check=True)
                    ins.then_inc(sems["pv"], 1)

                def turn_out(a, g):
                    pe.wait_ge(sems["sums_out"], at("sums_out", a, g + 1))
                    for q in range(C):
                        ins = pe.transpose(po[:, q * P:(q + 1) * P], OTs[:, q * P:(q + 1) * P], ident[:, :])
                    ins.then_inc(sems["sums_turned"], 1)

                def project_turn(a, q):
                    if q == 0:
                        pe.wait_ge(sems["heads_normed"], at("heads_normed", a, G))
                    for kt in range(KE):
                        ins = pe.transpose(ps[q % 2][:, kt * P:(kt + 1) * P], On[:, q, :, :].rearrange("p h d -> p (h d)")[:, kt * P:(kt + 1) * P], ident[:, :])
                    ins.then_inc(sems["heads_turned"], 1)

                def project(a, q):
                    pe.wait_ge(sems["heads_copied"], at("heads_copied", a, q + 1))
                    if q >= 2:
                        pe.wait_ge(sems["x2_rows"], at("x2_rows", a, q - 1))
                    for kt in range(KE):
                        ins = mm(pt[q % 2][:, 0:E], OnT[:, q % 2, kt, :], wo[:, kt, :], kt == 0, kt == KE - 1)
                    ins.then_inc(sems["projected"], 1)

                def body(b, a, nxt):
                    for u in range(SLOTS):
                        if a is not None:
                            if u < UNITS:
                                score(a, u)
                            if 2 <= u < UNITS + 2:
                                turn(a, u - 2)
                            if u >= 18 and (u - 18) % UG == 0 and (u - 18) // UG < G:
                                pv(a, (u - 18) // UG)
                            if u >= 19 and (u - 19) % UG == 0 and (u - 19) // UG < G:
                                turn_out(a, (u - 19) // UG)
                            if UNITS + 4 <= u < UNITS + 4 + C:
                                project_turn(a, u - UNITS - 4)
                                project(a, u - UNITS - 4)
                        for stg in WHEN["pe"][u]:
                            mb = nxt if stg[0] in HEAD else b
                            if mb is not None:
                                m(stg, mb)

                batches(pe, body)

                for m_ in range(PAIRS + 1):
                    if m_ < PAIRS:
                        pe.wait_ge(step["f_normed"], 2 * (m_ + 1))
                        pe.wait_ge(step["f_copied"], max(0, m_ - 1))
                        for q in range(2 * KE):
                            ins = pe.transpose(pt[m_ % 2][:, q * P:(q + 1) * P], n_f[:, m_ % 2, q * P:(q + 1) * P], ident[:, :])
                        ins.then_inc(step["f_turned"], 1)
                    if m_:
                        w = m_ - 1
                        pe.wait_ge(step["f_placed"], P // SEG * (w // (B // 2) + 1))
                        pe.wait_ge(step["f_copied"], w + 1)
                        pe.wait_ge(step["f_sum"], max(0, w - 1))
                        for h in range(2):
                            for kt in range(KE):
                                for j in range(P // SEG):
                                    ins = pe.matmul(ps[w % 2][SEG * j:SEG * (j + 1), h * E:(h + 1) * E],
                                                    t_f[:, w % 2, (h * KE + kt) * P + SEG * j:(h * KE + kt) * P + SEG * (j + 1)],
                                                    seg_w[w // (B // 2) % 2][:, j, kt, :],
                                                    start=(kt == 0), stop=(kt == KE - 1), tile_position=(0, SEG * j), skip_group_check=True)
                        ins.then_inc(step["f_product"], 1)

            @block.scalar
            def _(act):
                act.wait_ge(route_loads, 16 * 3)
                act.activation(sig_e, sig_e, ACT.Sign).then_inc(step["f_signs"], 1)
                act.wait_ge(consts, CONSTS)
                act.activation(nega[:, :], alog[:, :], ACT.Exp).then_inc(setup["act"], 1)
                act.wait_ge(setup["act"], 1)
                act.mul(nega[:, :], nega[:, :], -1.0).then_inc(setup["ready"], 1)
                act.wait_ge(setup["ready"], 3)

                def m(stg, b):
                    k = stg[0]
                    if k == "lnT":
                        for kt in range(KE):
                            act.wait_ge(full(("lnT", kt)), full_at(("lnT", kt), b))
                            act.activation(xnT[:, kt, :], bank(("lnT", kt))[:, :], ACT.Identity, bias=lnb[:, kt:kt + 1], scale=lnw[:, kt:kt + 1]).then_inc(read(("lnT", kt)), 1)
                    if k == "dt1":
                        act.wait_ge(sems["dt_step"], at("dt_step", b, 2))
                        act.activation(dts[:, 2, :, :], dts[:, 1, :, :], ACT.Exp, scale=-1.0).then_inc(sems["dt_exp"], 1)
                    if k == "bc":
                        act.wait_ge(full(stg), full_at(stg, b))
                        i = mt_order(stg[1])
                        if i >= PRE:
                            act.wait_ge(sems[conv_by(CONV_ORDER[i - PRE])], at(conv_by(CONV_ORDER[i - PRE]), b, taps_at(CONV_ORDER[i - PRE], DC)))
                        else:
                            act.wait_ge(sems[conv_by(CONV_ORDER[i - PRE])], at(conv_by(CONV_ORDER[i - PRE]), b - 1, taps_at(CONV_ORDER[i - PRE], DC)))
                        act.copy(pre[:, i % PRE, DC - 1:], bank(stg)[:, :]).then_inc(read(stg), 1)
                    if k == "z":
                        act.wait_ge(full(stg), full_at(stg, b))
                        if stg[1] == 0:
                            act.wait_ge(sems["k_low"], at("k_low", b, 2))
                        if stg[1] >= 2:
                            act.wait_ge(read(("z", stg[1] - 2)), read_at(("z", stg[1] - 2), b))
                        act.activation(zt[:, stg[1] % 2, :], bank(stg)[:, :], ACT.Tanh, scale=0.5).then_inc(sems["z_tanh"], 1)
                    if k == "cum":
                        act.wait_ge(full(("cum",)), full_at(("cum",), b))
                        act.activation(ecum[:, :, :, :].rearrange("p a c h -> p (a c h)"), bank(("cum",))[:, 0:2 * C * NH], ACT.Exp).then_inc(read(("cum",)), 1)
                    if k == "k":
                        act.wait_ge(sems["q_low"], at("q_low", b, 0))
                        for ct in range(KE):
                            act.wait_ge(full(("k", ct)), full_at(("k", ct), b))
                            act.activation(kf[:, ct, :], bank(("k", ct))[:, :], ACT.Identity, bias=bk[:, ct:ct + 1]).then_inc(read(("k", ct)), 1)
                    if k == "seg":
                        c = stg[1]
                        if c:
                            act.wait_ge(full(("intra", c - 1)), full_at(("intra", c - 1), b))
                        else:
                            act.wait_ge(full(("intra", C - 1)), full_at(("intra", C - 1), b - 1))
                        for j in range(2):
                            act.wait_ge(full(("seg", j, c)), full_at(("seg", j, c), b))
                            act.activation(L[:, 4 * j:4 * j + 4, :].rearrange("p h i -> p (h i)"), bank(("seg", j, c))[:, :], ACT.Exp).then_inc(read(("seg", j, c)), 1)
                    if k == "gx":
                        c = stg[1]
                        act.wait_ge(full(("xt", c)), full_at(("xt", c), b))
                        if c:
                            act.wait_ge(read(("intra", c - 1)), read_at(("intra", c - 1), b))
                        act.copy(xt[:, :, :].rearrange("p h d -> p (h d)"), bank(("xt", c))[:, :]).then_inc(read(("xt", c)), 1)
                    if k == "gate":
                        c = stg[1]
                        act.wait_ge(sems["y_gated"], at("y_gated", b, c + 1))
                        act.activation(th[:, 0, :], yg[:, :, :].rearrange("p h d -> p (h d)"), ACT.Square, accum_out=ss[:, :]).then_inc(sems["sumsq"], 1)
                    if k == "o":
                        c = stg[1]
                        act.wait_ge(full(("yT", c)), full_at(("yT", c), b))
                        act.copy(ygT[:, :, :].rearrange("p k i -> p (k i)"), bank(("yT", c))[:, :]).then_inc(read(("yT", c)), 1)
                    if k == "silu":
                        silu(b, stg[1])
                    if k == "q1":
                        for kt in range(KE):
                            act.wait_ge(full(("xqT", kt)), full_at(("xqT", kt), b))
                            act.copy(xqT[:, kt, :], bank(("xqT", kt))[:, :]).then_inc(read(("xqT", kt)), 1)
                    if k == "q2":
                        act.wait_ge(sems["k_low"], at("k_low", b, 2))
                        for ct in range(KE):
                            act.wait_ge(full(("q", ct)), full_at(("q", ct), b))
                            act.activation(qf[:, ct, :], bank(("q", ct))[:, :], ACT.Identity, bias=bq[:, ct:ct + 1], scale=AD ** -0.5).then_inc(read(("q", ct)), 1)

                def silu(b, mt):
                    act.wait_ge(sems[conv_by(mt)], at(conv_by(mt), b, taps_at(mt, DC)))
                    act.wait_ge(sems["silu"], at("silu", b, mt_order(mt) - 1))
                    act.activation(th[:, mt_order(mt) % 2, :], xc[:, mt, :], ACT.Tanh).then_inc(sems["tanh"], 1)

                def exp(a, u):
                    act.wait_ge(sems["row_max"], at("row_max", a, u + 1))
                    act.wait_ge(sems["turned"], at("turned", a, u - 1))
                    act.activation(Pr[:, u % 2, :], T[:, u % 2, :], ACT.Exp, bias=nmx[:, u % 2:u % 2 + 1], scale=-1.0).then_inc(sems["probs"], 1)

                def body(b, a, nxt):
                    for u in range(SLOTS):
                        if a is not None:
                            if u < UNITS:
                                exp(a, u)
                            if 2 <= u < UNITS + 2 and u % 2 == 0:
                                g, qt, hh = unit(u - 2)
                                act.wait_ge(sems["turned"], at("turned", a, u - 1))
                                act.wait_ge(sems["pv"], at("pv", a, g))
                                act.copy(PT[:, hh, :, qt * P:(qt + 1) * P], pt[u % 2][:, :].rearrange("p (k i) -> p k i", i=P)).then_inc(sems["evac_act"], 1)
                            if u >= 18 and (u - 18) % UG == 0 and (u - 18) // UG < G:
                                g = (u - 18) // UG
                                act.wait_ge(sems["pv"], at("pv", a, g + 1))
                                act.copy(OTs[:, :], po[:, :]).then_inc(sems["sums_out"], 1)
                            if UNITS + 4 <= u < UNITS + 4 + C:
                                q = u - UNITS - 4
                                act.wait_ge(sems["heads_turned"], at("heads_turned", a, q + 1))
                                act.wait_ge(sems["projected"], at("projected", a, q - 1))
                                act.copy(OnT[:, q % 2, :, :].rearrange("p k i -> p (k i)"), ps[q % 2][:, 0:KE * P]).then_inc(sems["heads_copied"], 1)
                        for stg in WHEN["act"][u]:
                            mb = nxt if stg[0] in HEAD else b
                            if mb is not None:
                                m(stg, mb)

                batches(act, body)

                def place(k):
                    act.wait_ge(step["f_product"], B // 2 * max(0, k - 1))
                    for j in range(P // SEG):
                        expert = act.value_load(seg_expert[0:1, P // SEG * k + j:P // SEG * k + j + 1], min_val=0, max_val=NT - 1)
                        act.copy(seg_w[k % 2][:, j, :, :], w_f[:, :, bass.ds(expert, 1), :].rearrange("p k o e -> p k (o e)")).then_inc(step["f_placed"], 1)

                act.wait_ge(step["f_rows"], 1)
                act.wait_ge(step["f_w"], 16)
                place(0)
                place(1)
                for m_ in range(PAIRS):
                    if m_ % (B // 2) == 2 and 1 < m_ // (B // 2) + 1 < BLOCKS:
                        place(m_ // (B // 2) + 1)
                    act.wait_ge(step["f_turned"], m_ + 1)
                    act.wait_ge(step["f_product"], max(0, m_ - 1))
                    act.copy(t_f[:, m_ % 2, :], pt[m_ % 2][:, :]).then_inc(step["f_copied"], 1)

            def route(dve):
                done = [0]

                def then(ins):
                    ins.then_inc(step["f_routed"], 1)
                    done[0] += 1
                    dve.wait_ge(step["f_routed"], done[0])

                def view(at_, *shape):
                    n = int(np.prod(shape))
                    ap = tmp[:, at_:at_ + n]
                    return ap.rearrange("p (a b) -> p a b", b=shape[-1]) if len(shape) == 2 else (
                        ap.rearrange("p (a b c) -> p a b c", b=shape[1], c=shape[2]) if len(shape) == 3 else ap)

                def over(ap, shape, axis):
                    letters = {1: "p (o a) -> p o a", 2: "p (a o) -> p a o"}[axis]
                    return ap.rearrange(letters, o=1).broadcast_to(shape)

                oh = view(OH, C, NT)
                sc, key = view(ST, C, NT), view(ST + 32, C, NT)
                best, top = view(ST + 64, C), view(ST + 68, C)
                dve.wait_ge(route_loads, 16 * 3)
                dve.wait_ge(step["f_scores"], 1)
                scores = po[:, 0:C * NT].rearrange("p (c t) -> p c t", t=NT)
                then(dve.tensor_reduce(best, scores, AX.X, ALU.max))
                then(dve.tensor_tensor(sc, scores, over(best, [P, C, NT], 2), ALU.is_equal))
                then(dve.tensor_tensor(key, sc, over(rcol["first"], [P, C, NT], 1), ALU.mult))
                then(dve.tensor_reduce(top, key, AX.X, ALU.max))
                dve.tensor_tensor(oh, key, over(top, [P, C, NT], 2), ALU.is_equal).then_inc(step["f_onehot"], 1)
                dve.wait_ge(step["f_counts"], 1)
                n_at = S // SEG
                many, segs = view(RIGHT + 24, NT, n_at), view(ST + 72, NT)
                count, starts, ends = view(ST + 100, NT), view(ST + 108, NT), view(ST + 116, NT)
                then(dve.tensor_copy(count, po[:, C * NT:(C + 1) * NT]))
                then(dve.tensor_tensor(many, over(count, [P, NT, n_at], 2), over(rcol["seg_at"], [P, NT, n_at], 1), ALU.is_gt))
                then(dve.tensor_reduce(segs, many, AX.X, ALU.add))
                before = view(ST + 130, NT, NT)
                then(dve.tensor_tensor(before, over(segs, [P, NT, NT], 1), rcol["before"].rearrange("p (a b) -> p a b", b=NT), ALU.mult))
                then(dve.tensor_reduce(starts, before, AX.X, ALU.add))
                then(dve.tensor_tensor(ends, starts, segs, ALU.add))
                rank, slot = view(ST + 200, C, NT), view(ST + 232, C)
                then(dve.scalar_tensor_tensor(rank, over(starts, [P, C, NT], 1), float(SEG), po[:, 0:C * NT].rearrange("p (c t) -> p c t", t=NT), ALU.mult, ALU.add))
                then(dve.tensor_tensor(rank, rank, oh, ALU.mult))
                then(dve.tensor_reduce(slot, rank, AX.X, ALU.add))
                then(dve.tensor_scalar(slot, slot, -1.0, None, ALU.add))
                past, block, place = view(ST + 240, C, BLOCKS - 1), view(ST + 262, C), view(ST + 268, C)
                then(dve.tensor_tensor(past, over(slot, [P, C, BLOCKS - 1], 2), over(rcol["block_at"], [P, C, BLOCKS - 1], 1), ALU.is_ge))
                then(dve.tensor_reduce(block, past, AX.X, ALU.add))
                then(dve.scalar_tensor_tensor(place, block, -float(P), slot, ALU.mult, ALU.add))
                left, right = view(LEFT, C, P), view(RIGHT, C, BLOCKS)
                then(dve.tensor_tensor(left, over(rcol["slot"], [P, C, P], 1), over(place, [P, C, P], 2), ALU.is_equal))
                then(dve.tensor_tensor(right, over(rcol["blk"], [P, C, BLOCKS], 1), over(block, [P, C, BLOCKS], 2), ALU.is_equal))
                dve.tensor_tensor(right, right, over(rcol["pos1"], [P, C, BLOCKS], 2), ALU.mult).then_inc(step["f_tables"], 1)
                seg_n, slot_n = view(ST + 280, SEGS, NT), view(ST + 480, BLOCKS, NT)
                seg_f, slot_f = view(ST + 540, SEGS), view(ST + 570, BLOCKS)
                then(dve.tensor_tensor(seg_n, over(ends, [P, SEGS, NT], 1), over(rcol["seg"], [P, SEGS, NT], 2), ALU.is_le))
                then(dve.tensor_reduce(seg_f, seg_n, AX.X, ALU.add))
                then(dve.tensor_scalar(seg_f, seg_f, float(NT - 1), None, ALU.min))
                then(dve.tensor_copy(seg_expert[0:1, :], seg_f[0:1, :]))
                then(dve.tensor_tensor(slot_n, over(ends, [P, BLOCKS, NT], 1), over(rcol["blk_slot"], [P, BLOCKS, NT], 2), ALU.is_le))
                then(dve.tensor_reduce(slot_f, slot_n, AX.X, ALU.add))
                then(dve.tensor_scalar(slot_f, slot_f, float(NT - 1), None, ALU.min))
                then(dve.tensor_copy(expert_of[:, :], slot_f))
                dve.wait_ge(step["f_slots"], 1)
                held, empty = view(ST + 580, BLOCKS), view(ST + 590, BLOCKS)
                then(dve.tensor_scalar(empty, po[:, 0:BLOCKS], 0.0, 1e6, ALU.is_equal, ALU.mult))
                then(dve.scalar_tensor_tensor(held, po[:, 0:BLOCKS], -1.0, empty, ALU.add, ALU.add))
                dve.tensor_copy(row_of[:, :], held).then_inc(step["f_rows"], 1)

            @block.vector
            def _(dve):
                dve.memset(nhalf[:, :], -0.5).then_inc(setup["dve"], 1)
                dve.memset(ones[:, :], 1.0).then_inc(setup["dve"], 1)
                dve.memset(vm[:, :, :, :], 0.0).then_inc(setup["dve"], 1)
                dve.memset(q_st[:, :, :, :].bitcast(F32), 0.0).then_inc(setup["dve"], 1)
                dve.memset(k_st[:, :, :, :].bitcast(F32), 0.0).then_inc(setup["dve"], 1)
                dve.wait_ge(setup["dve"], 5)
                dve.memset(vm[:, :, :, AD:AD + 1], 1.0).then_inc(setup["dve"], 1)
                dve.wait_ge(consts, CONSTS)
                dve.tensor_scalar(cw[:, :, :], cw[:, :, :], 0.5, None, ALU.mult).then_inc(setup["dve"], 1)
                dve.tensor_scalar(cb[:, :], cb[:, :], 0.5, None, ALU.mult).then_inc(setup["dve"], 1)
                dve.tensor_scalar(bq[:, :], bq[:, :], AD ** -0.5, None, ALU.mult).then_inc(setup["dve"], 1)
                for kt in range(KI):
                    dve.tensor_scalar(wout[:, kt, :], wout[:, kt, :], nw[:, kt:kt + 1], 0.5, ALU.mult, ALU.mult).then_inc(setup["dve"], 1)
                dve.wait_ge(setup["dve"], 9 + KI)
                dve.memset(pre[:, :, 0:DC - 1], 0.0).then_inc(setup["ready"], 1)
                dve.wait_ge(setup["ready"], 3)
                route(dve)

                def m(stg, b):
                    k = stg[0]
                    if k == "ln1":
                        dve.wait_ge(sems["x_loaded"], at("x_loaded", b, 16))
                        for c in range(C):
                            dve.bn_stats(st[:, c, :], x_in[:, c, :]).then_inc(sems["stats"], 1)
                        dve.wait_ge(sems["ln_x"], at("ln_x", b, 0))
                        for c in range(C):
                            dve.wait_ge(*alone(dve, sems["stats"], at("stats", b, c + 1)))
                            dve.bn_aggr(mv[:, c, :], st[:, c, :]).then_inc(sems["mean_var"], 1)
                        dve.wait_ge(sems["mean_var"], at("mean_var", b, C))
                        dve.tensor_scalar(ve[:, :, 0:1], mv[:, :, 1:2], EPS, None, ALU.add).then_inc(sems["var_eps"], 1)
                        dve.tensor_scalar(ve[:, :, 1:2], mv[:, :, 1:2], 1.0 + EPS, EPS * EPS, ALU.mult, ALU.add).then_inc(sems["var_eps"], 1)
                    if k == "ln2":
                        dve.wait_ge(sems["rstd"], at("rstd", b, 1))
                        for c in range(C):
                            dve.tensor_scalar(xn[:, c, :], x_in[:, c, :], mv[:, c, 0:1], rs[:, c, 1:2], ALU.subtract, ALU.mult).then_inc(sems["normed"], 1)
                    if k == "dt1":
                        dve.wait_ge(full(("dt",)), full_at(("dt",), b))
                        dve.tensor_tensor(dts[:, 0, :, :], bank(("dt",))[:, 0:C * NH].rearrange("p (c h) -> p c h", h=NH), dtb[:, :, :], ALU.add).then_inc(read(("dt",)), 1)
                        dve.wait_ge(read(("dt",)), read_at(("dt",), b))
                        n = 0

                        def step(ins):
                            ins.then_inc(sems["dt_step"], 1)

                        step(dve.tensor_scalar(dts[:, 3, :, :], dts[:, 0, :, :], 0.0, None, ALU.max))
                        step(dve.scalar_tensor_tensor(dts[:, 1, :, :], dts[:, 0, :, :], -1.0, dts[:, 0, :, :], ALU.mult, ALU.max))
                    if k == "dt2":
                        e, r, y, y2, acc = (dts[:, i, :, :] for i in (2, 4, 5, 6, 7))
                    if stg == ("dt2", 0):
                        dve.wait_ge(sems["dt_exp"], at("dt_exp", b, 1))
                        dve.tensor_scalar(r, e, 2.0, None, ALU.add).then_inc(sems["dt_step"], 1)
                        dve.wait_ge(sems["dt_step"], at("dt_step", b, 3))
                        dve.reciprocal(y, r).then_inc(sems["dt_step"], 1)
                        dve.wait_ge(sems["dt_step"], at("dt_step", b, 4))
                        dve.tensor_tensor(y, y, e, ALU.mult).then_inc(sems["dt_step"], 1)
                    if stg == ("dt2", 1):
                        dve.wait_ge(sems["dt_step"], at("dt_step", b, 5))
                        dve.tensor_tensor(y2, y, y, ALU.mult).then_inc(sems["dt_step"], 1)
                        dve.wait_ge(sems["dt_step"], at("dt_step", b, 6))
                        dve.tensor_scalar(acc, y2, 1.0 / 15, None, ALU.mult).then_inc(sems["dt_step"], 1)
                    if stg in (("dt2", 1), ("dt2", 2)):
                        for i, d in ((0, 13), (1, 11)) if stg[1] == 1 else ((2, 9), (3, 7), (4, 5)):
                            dve.wait_ge(sems["dt_step"], at("dt_step", b, 7 + i))
                            dve.scalar_tensor_tensor(acc, acc, 1.0 / d, y2, ALU.add, ALU.mult).then_inc(sems["dt_step"], 1)
                    if stg == ("dt2", 3):
                        dve.wait_ge(sems["dt_step"], at("dt_step", b, 12))
                        dve.scalar_tensor_tensor(acc, acc, 1.0 / 3, y2, ALU.add, ALU.mult).then_inc(sems["dt_series"], 1)
                        dve.wait_ge(sems["dt_series"], at("dt_series", b, 1))
                        dve.scalar_tensor_tensor(acc, acc, 1.0, y, ALU.add, ALU.mult).then_inc(sems["dt_series"], 1)
                        dve.wait_ge(sems["dt_series"], at("dt_series", b, 2))
                        dve.scalar_tensor_tensor(dt[:, :, :], acc, 2.0, dts[:, 3, :, :], ALU.mult, ALU.add).then_inc(sems["dt_ready"], 1)
                        dve.wait_ge(sems["dt_ready"], at("dt_ready", b, 1))
                        dve.tensor_tensor(dA[:, :, :], dt[:, :, :], nega[:, :].rearrange("p (o h) -> p o h", o=1).broadcast_to([P, C, NH]), ALU.mult).then_inc(sems["dt_ready"], 1)
                    if k == "z":
                        c = stg[1]
                        dve.wait_ge(sems["z_tanh"], at("z_tanh", b, c + 1))
                        dve.scalar_tensor_tensor(zs[:, :], zt[:, c % 2, :], 1.0, bank(stg)[:, :], ALU.add, ALU.mult).then_inc(read(stg), 1)
                    if k == "v":
                        for j in range(2):
                            dve.wait_ge(full(("v", j)), full_at(("v", j), b))
                            if j == 0:
                                dve.wait_ge(sems["va_moved"], at("va_moved", b, 0))
                            for i in range(2):
                                ins = dve.tensor_tensor(vm[:, 2 * j + i, :, 0:AD], bank(("v", j))[:, i * E:(i + 1) * E].rearrange("p (h d) -> p h d", d=AD),
                                                        bvb[:, :].rearrange("p (h d) -> p h d", d=AD), ALU.add)
                                if i == 0:
                                    ins.then_inc(sems["v_half"], 1)
                            ins.then_inc(read(("v", j)), 1)
                    if k == "am":
                        c = stg[1]
                        if c == 0:
                            dve.wait_ge(sems["mask_loaded"], at("mask_loaded", b, 16))
                        dve.tensor_scalar(am_m[:, c, :], am_m[:, c, :].bitcast(I32), 0, MASKED, ALU.is_equal, ALU.mult).then_inc(sems["mask_bias"], 1)
                    if k == "gx":
                        c = stg[1]
                        dve.wait_ge(full(("gb", c)), full_at(("gb", c), b))
                        dve.tensor_tensor(Gm[:, :], bank(("gb", c))[:, 0:P], triu[:, :], ALU.mult).then_inc(sems["gram_masked"], 1)
                        dve.tensor_copy(Bt[:, :], bank(("gb", c))[:, P:2 * P]).then_inc(read(("gb", c)), 1)
                    if k == "w":
                        c = stg[1]
                        for j in range(2):
                            dve.wait_ge(read(("seg", j, c)), read_at(("seg", j, c), b))
                        dve.wait_ge(sems["gram_masked"], at("gram_masked", b, c + 1))
                        if c < C - 1:
                            dve.wait_ge(sems["x_decayed"], at("x_decayed", b, c + 1))
                        dve.tensor_tensor(L[:, :, :], L[:, :, :], Gm[:, :].rearrange("p (o i) -> p o i", o=1).broadcast_to([P, NH, P]), ALU.mult).then_inc(sems["weights"], 1)
                    if k == "y":
                        c = stg[1]
                        v3 = lambda ap: ap.rearrange("p (h d) -> p h d", d=HD)
                        dve.wait_ge(sems["x_D"], at("x_D", b, c + 1))
                        if c:
                            dve.wait_ge(full(("inter", c)), full_at(("inter", c), b))
                            dve.wait_ge(read(("cum",)), read_at(("cum",), b))
                            dve.tensor_tensor(ti[:, :, :], v3(bank(("inter", c))[:, :]), ecum[:, 0, c, :].rearrange("p (h o) -> p h o", o=1).broadcast_to([P, NH, HD]), ALU.mult).then_inc(read(("inter", c)), 1)
                            dve.wait_ge(read(("inter", c)), read_at(("inter", c), b))
                            dve.tensor_tensor(ti[:, :, :], ti[:, :, :], xD[:, :, :], ALU.add).then_inc(sems["y_inter"], 1)
                            dve.wait_ge(sems["y_inter"], at("y_inter", b, c))
                        dve.wait_ge(full(("intra", c)), full_at(("intra", c), b))
                        src = ti if c else xD
                        dve.tensor_tensor(ti[:, :, :], v3(bank(("intra", c))[:, :]), src[:, :, :], ALU.add).then_inc(read(("intra", c)), 1)
                        if c < C - 1:
                            dve.wait_ge(full(("state", c)), full_at(("state", c), b))
                            if c:
                                dve.wait_ge(sems["state_decayed"], at("state_decayed", b, c))
                                dve.tensor_tensor(state[:, :, :], v3(bank(("state", c))[:, :]), sdec[:, :, :], ALU.add).then_inc(read(("state", c)), 1)
                            else:
                                dve.tensor_copy(state[:, :, :], v3(bank(("state", c))[:, :])).then_inc(read(("state", c)), 1)
                    if k == "gate":
                        c = stg[1]
                        dve.wait_ge(read(("intra", c)), read_at(("intra", c), b))
                        dve.wait_ge(read(("z", c)), read_at(("z", c), b))
                        dve.tensor_tensor(yg[:, :, :], ti[:, :, :], zs[:, :].rearrange("p (h d) -> p h d", d=HD), ALU.mult).then_inc(sems["y_gated"], 1)
                    if k == "gate2":
                        c = stg[1]
                        dve.wait_ge(sems["sumsq"], at("sumsq", b, c + 1))
                        dve.tensor_scalar(se[:, :], ss[:, :], 0.25 / DI, EPS, ALU.mult, ALU.add).then_inc(sems["meansq"], 1)
                    if k == "x1":
                        c = stg[1]
                        dve.wait_ge(full(("out", c)), full_at(("out", c), b))
                        dve.wait_ge(sems["gate_rstd"], at("gate_rstd", b, c + 1))
                        dve.scalar_tensor_tensor(x1[:, c, :], bank(("out", c))[:, 0:E], rr[:, 0:1], xr[:, c, :], ALU.mult, ALU.add).then_inc(read(("out", c)), 1)
                        dve.wait_ge(read(("out", c)), read_at(("out", c), b))
                        dve.bn_stats(st2[:, :], x1[:, c, :]).then_inc(sems["stats2"], 1)
                        dve.wait_ge(*alone(dve, sems["stats2"], at("stats2", b, c + 1)))
                        dve.bn_aggr(mv2[:, :], st2[:, :]).then_inc(sems["mean_var2"], 1)
                        dve.wait_ge(sems["mean_var2"], at("mean_var2", b, c + 1))
                        dve.tensor_scalar(ve2[:, :], mv2[:, 1:2], EPS, None, ALU.add).then_inc(sems["var_eps2"], 1)
                    if k == "xq":
                        c = stg[1]
                        dve.wait_ge(sems["rstd2"], at("rstd2", b, c + 1))
                        dve.tensor_scalar(xq[:, c, :], x1[:, c, :], mv2[:, 0:1], r2[:, 0:1], ALU.subtract, ALU.mult).then_inc(sems["query_normed"], 1)
                    if k == "silu":
                        silu(b, stg[1])
                    if k == "conv" and stg[1] in ON_DVE:
                        conv(b, stg[1])
                    if k == "q2" or k == "k":
                        n = "q" if k == "q2" else "k"
                        if k == "k":
                            dve.wait_ge(sems["qk_out"], at("qk_out", b, 0))
                        else:
                            dve.wait_ge(sems["qk_out"], at("qk_out", b, 16 * 4))
                        for ct in range(KE):
                            dve.wait_ge(read((n, ct)), read_at((n, ct), b))
                            dve.tensor_copy(kp[:, 0, ct, :], kf[:, ct, :]).then_inc(sems[f"{n}_high"], 1)
                        for ct in range(KE):
                            dve.wait_ge(sems[f"{n}_high"], at(f"{n}_high", b, ct + 1))
                            dve.tensor_tensor(kp[:, 1, ct, :], kf[:, ct, :], kp[:, 0, ct, :].bitcast(F32), ALU.subtract).then_inc(sems[f"{n}_low"], 1)

                def conv(b, mt):
                    src = pre[:, mt_order(mt) % PRE, :]
                    dve.wait_ge(read(("bc", mt)), read_at(("bc", mt), b))
                    dve.tensor_scalar(xc[:, mt, :], src[:, 0:S], cw[:, mt, 0:1], cb[:, mt:mt + 1], ALU.mult, ALU.add).then_inc(sems["conv_dve"], 1)
                    for j in range(1, DC):
                        dve.wait_ge(sems[conv_by(mt)], at(conv_by(mt), b, taps_at(mt, j)))
                        dve.scalar_tensor_tensor(xc[:, mt, :], src[:, j:j + S], cw[:, mt, j:j + 1], xc[:, mt, :], ALU.mult, ALU.add).then_inc(sems["conv_dve"], 1)

                def silu(b, mt):
                    i = mt_order(mt)
                    dve.wait_ge(sems["tanh"], at("tanh", b, i + 1))
                    dve.scalar_tensor_tensor(xc[:, mt, :], th[:, i % 2, :], 1.0, xc[:, mt, :], ALU.add, ALU.mult).then_inc(sems["silu"], 1)

                def take_max(a, u):
                    g, qt, hh = unit(u)
                    if u == 0:
                        dve.wait_ge(sems["bias_moved01"], at("bias_moved01", a, 16))
                    if u == 2:
                        dve.wait_ge(sems["bias_moved23"], at("bias_moved23", a, 16))
                    dve.wait_ge(*alone(dve, sems["score"], at("score", a, u + 1)))
                    dve.wait_ge(*alone(dve, sems["probs"], at("probs", a, u - 1)))
                    dve.tensor_tensor_reduce(T[:, u % 2, :], ps[u % 2][:, :], am[:, qt, :], -1.0, 3e38, ALU.add, ALU.min, nmx[:, u % 2:u % 2 + 1]).then_inc(sems["row_max"], 1)

                def body(b, a, nxt):
                    for u in range(SLOTS):
                        if a is not None:
                            if u < UNITS:
                                take_max(a, u)
                            if 2 <= u < UNITS + 2 and u % 2 == 1:
                                g, qt, hh = unit(u - 2)
                                dve.wait_ge(sems["turned"], at("turned", a, u - 1))
                                dve.wait_ge(sems["pv"], at("pv", a, g))
                                dve.tensor_copy(PT[:, hh, :, qt * P:(qt + 1) * P], pt[u % 2][:, :].rearrange("p (k i) -> p k i", i=P)).then_inc(sems["evac_dve"], 1)
                            if u >= 19 and (u - 19) % UG == 0 and (u - 19) // UG < G:
                                g = (u - 19) // UG
                                dve.wait_ge(sems["sums_turned"], at("sums_turned", a, g + 1))
                                po4 = po[:, :].rearrange("p (q h v) -> p q h v", q=C, h=HG)
                                dve.reciprocal(rden[:, :, :], po4[:, :, :, AD]).then_inc(sems["recip"], 1)
                                dve.wait_ge(sems["recip"], at("recip", a, g + 1))
                                for q in range(C):
                                    ins = dve.tensor_tensor(On[:, q, g * HG:(g + 1) * HG, :], po4[:, q, :, 0:AD],
                                                            rden[:, q, :].rearrange("p (h o) -> p h o", o=1).broadcast_to([P, HG, AD]), ALU.mult)
                                ins.then_inc(sems["heads_normed"], 1)
                            if UNITS + 4 <= u < UNITS + 4 + C:
                                q = u - UNITS - 4
                                dve.wait_ge(sems["projected"], at("projected", a, q + 1))
                                if q == 0:
                                    dve.wait_ge(sems["x1a_moved"], at("x1a_moved", a, 16))
                                dve.tensor_tensor(x1a[:, q, :], pt[q % 2][:, 0:E], x1a[:, q, :], ALU.add).then_inc(sems["x2_rows"], 1)
                        for stg in WHEN["dve"][u]:
                            mb = nxt if stg[0] in HEAD else b
                            if mb is not None:
                                m(stg, mb)

                batches(dve, body)

                def stats(k, rows):
                    if rows[0] == 0:
                        dve.wait_ge(f_in[k % BUFS], 16 * (k // BUFS + 1))
                        dve.wait_ge(step["f_normed"], B * max(0, k - 1))
                    for j in rows:
                        dve.bn_stats(st_f[:, k % 2, 6 * j:6 * (j + 1)], x_f[k % BUFS][:, j * E:(j + 1) * E]).then_inc(step["f_stats"], 1)
                    for j in rows:
                        dve.wait_ge(step["f_stats"], B * k + j + 1)
                        dve.bn_aggr(mv_f[:, k % 2, 2 * j:2 * j + 2], st_f[:, k % 2, 6 * j:6 * (j + 1)]).then_inc(step["f_mean_var"], 1)
                    if rows[-1] == B - 1:
                        dve.wait_ge(step["f_mean_var"], B * (k + 1))
                        dve.tensor_scalar(ve_f[:, k % 2, :].rearrange("p (j o) -> p j o", o=1), mv_f[:, k % 2, :].rearrange("p (j o) -> p j o", o=2)[:, :, 1:2], EPS, None, ALU.add).then_inc(step["f_var_eps"], 1)

                stats(0, range(B))
                for m_ in range(PAIRS + 2):
                    k, n = m_ // (B // 2), m_ % (B // 2)
                    if m_ < PAIRS:
                        dve.wait_ge(step["f_rstd"], k + 1)
                        dve.wait_ge(step["f_turned"], max(0, m_ - 1))
                        for j in (2 * n, 2 * n + 1):
                            dve.tensor_scalar(n_f[:, m_ % 2, j % 2 * E:(j % 2 + 1) * E], x_f[k % BUFS][:, j * E:(j + 1) * E], mv_f[:, k % 2, 2 * j:2 * j + 1], r_f[:, k % 2, j:j + 1],
                                              ALU.subtract, ALU.mult).then_inc(step["f_normed"], 1)
                        if k + 1 < BLOCKS:
                            stats(k + 1, (2 * n, 2 * n + 1))
                    if m_ >= 2:
                        w = m_ - 2
                        dve.wait_ge(step["f_biased"], w + 1)
                        dve.wait_ge(step["f_product"], w + 1)
                        two = x_f[w // (B // 2) % BUFS][:, w % (B // 2) * 2 * E:(w % (B // 2) + 1) * 2 * E]
                        dve.tensor_tensor(two, ps[w % 2][:, :], two, ALU.add).then_inc(step["f_sum"], 1)

            @block.gpsimd
            def _(pool):
                pool.wait_ge(consts, CONSTS)
                pool.memset(state[:, :, :], 0.0).then_inc(setup["ready"], 1)
                pool.wait_ge(setup["ready"], 3)

                def conv(b, mt):
                    src, n = pre[:, mt_order(mt) % PRE, :], ON_POOL.index(mt)
                    pool.wait_ge(*alone(pool, read(("bc", mt)), read_at(("bc", mt), b)))
                    pool.tensor_scalar(xc[:, mt, :], src[:, 0:S], cw[:, mt, 0:1], cb[:, mt:mt + 1], ALU.mult, ALU.add).then_inc(sems["conv_pool"], 1)
                    for j in range(1, DC):
                        if j > 1 or n:
                            pool.wait_ge(*alone(pool, sems[conv_by(ON_POOL[n if j > 1 else n - 1])], at(conv_by(ON_POOL[n if j > 1 else n - 1]), b, taps_at(ON_POOL[n if j > 1 else n - 1], j if j > 1 else DC))))
                        pool.tensor_scalar(tap[:, :, :].rearrange("p k i -> p (k i)"), src[:, j:j + S], cw[:, mt, j:j + 1], 0.0, ALU.mult, ALU.add).then_inc(sems["tap_product"], 1)
                        pool.wait_ge(sems[conv_by(mt)], at(conv_by(mt), b, taps_at(mt, j)))
                        pool.wait_ge(sems["tap_product"], at("tap_product", b, (DC - 1) * n + j))
                        pool.tensor_tensor(xc[:, mt, :], xc[:, mt, :], tap[:, :, :].rearrange("p k i -> p (k i)"), ALU.add).then_inc(sems["conv_pool"], 1)

                def m(stg, b):
                    k = stg[0]
                    if k == "ln1":
                        pool.wait_ge(sems["var_eps"], at("var_eps", b, 2))
                        pool.tensor_tensor(rs[:, :, :].rearrange("p c k -> p (c k)"), ve[:, :, :].rearrange("p c k -> p (c k)"), nhalf[:, 0:2 * C], ALU.pow).then_inc(sems["rstd"], 1)
                    if k == "ln2":
                        pool.wait_ge(*alone(pool, sems["rstd"], at("rstd", b, 1)))
                        for c in range(C):
                            pool.tensor_scalar(xr[:, c, :], x_in[:, c, :], mv[:, c, 0:1], rs[:, c, 0:1], ALU.subtract, ALU.mult).then_inc(sems["ln_x"], 1)
                        pool.wait_ge(sems["ln_x"], at("ln_x", b, C))
                        pool.tensor_tensor(xr[:, :, :], x_in[:, :, :], xr[:, :, :], ALU.add).then_inc(sems["residual"], 1)
                    if k == "conv" and stg[1] in ON_POOL:
                        conv(b, stg[1])
                    if stg == ("am", C - 1):
                        pool.wait_ge(*alone(pool, sems["mask_bias"], at("mask_bias", b, C)))
                        pool.dma_start(am_m[:, :, :], t["adj"].rearrange("(c p) s -> p c s", p=P), accum_op=ALU.add).then_inc(sems["score_bias"], 16)
                    if k == "seg":
                        c = stg[1]
                        pool.wait_ge(sems["dt_ready"], at("dt_ready", b, 2))
                        pool.wait_ge(full(("intra", c - 1 if c else C - 1)), full_at(("intra", c - 1 if c else C - 1), b if c else b - 1))
                        pool.tensor_tensor(dmask[:, :, :], triu[:, :].rearrange("p (o i) -> p o i", o=1).broadcast_to([P, NH, P]),
                                           dA[:, c, :].rearrange("p (h o) -> p h o", o=1).broadcast_to([P, NH, P]), ALU.mult).then_inc(sems["decay_mask"], 1)
                    if k == "gx":
                        c = stg[1]
                        pool.wait_ge(read(("xt", c)), read_at(("xt", c), b))
                        if c:
                            pool.wait_ge(full(("intra", c - 1)), full_at(("intra", c - 1), b))
                            pool.wait_ge(sems["y_gated"], at("y_gated", b, c))
                        pool.tensor_tensor(xdt[:, :, :], xt[:, :, :], dt[:, c, :].rearrange("p (h o) -> p h o", o=1).broadcast_to([P, NH, HD]), ALU.mult).then_inc(sems["x_dt"], 1)
                        if c < C - 1:
                            if c:
                                pool.wait_ge(full(("state", c - 1)), full_at(("state", c - 1), b))
                            pool.wait_ge(sems["x_dt"], at("x_dt", b, c + 1))
                            for j in range(2):
                                pool.wait_ge(read(("seg", j, c)), read_at(("seg", j, c), b))
                            pool.tensor_tensor(xw[:, :, :], xdt[:, :, :], L[:, :, P - 1:P].broadcast_to([P, NH, HD]), ALU.mult).then_inc(sems["x_decayed"], 1)
                        pool.wait_ge(sems["x_dt"], at("x_dt", b, c + 1))
                        pool.tensor_tensor(xD[:, :, :], xt[:, :, :], dsk[:, :].rearrange("p (h o) -> p h o", o=1).broadcast_to([P, NH, HD]), ALU.mult).then_inc(sems["x_D"], 1)
                    if k == "y":
                        c = stg[1]
                        if 0 < c < C - 1:
                            pool.wait_ge(full(("inter", c)), full_at(("inter", c), b))
                            pool.wait_ge(read(("state", c - 1)), read_at(("state", c - 1), b))
                            if read(("cum",)) is not read(("state", c - 1)):
                                pool.wait_ge(read(("cum",)), read_at(("cum",), b))
                            pool.tensor_tensor(sdec[:, :, :], state[:, :, :], ecum[:, 1, c, :].rearrange("p (h o) -> p h o", o=1).broadcast_to([P, NH, HD]), ALU.mult).then_inc(sems["state_decayed"], 1)
                    if k == "gate2":
                        c = stg[1]
                        pool.wait_ge(sems["meansq"], at("meansq", b, c + 1))
                        pool.tensor_tensor(rr[:, :], se[:, :], nhalf[:, 0:1], ALU.pow).then_inc(sems["gate_rstd"], 1)
                    if k == "x1":
                        c = stg[1]
                        pool.wait_ge(sems["var_eps2"], at("var_eps2", b, c + 1))
                        pool.tensor_tensor(r2[:, :], ve2[:, :], nhalf[:, 0:1], ALU.pow).then_inc(sems["rstd2"], 1)
                    if k == "xq":
                        c = stg[1]
                        pool.wait_ge(sems["query_normed"], at("query_normed", b, c + 1))
                        pool.tensor_tensor(x1b[:, c, :], x1[:, c, :], bob[:, :], ALU.add).then_inc(sems["x1_bias"], 1)

                def body(b, a, nxt):
                    for u in range(SLOTS):
                        for stg in WHEN["pool"][u]:
                            mb = nxt if stg[0] in HEAD else b
                            if mb is not None:
                                m(stg, mb)

                batches(pool, body)

                def gather(k):
                    pool.indirect_dma_start(x_f[k % BUFS], None, x2_d, bass.IndirectOffsetOnAxis(row_of[:, k:k + 1].bitcast(U32), 0),
                                            bounds_check=S - 1, oob_is_err=False).then_inc(f_in[k % BUFS], 16)

                pool.wait_ge(step["f_rows"], 1)
                pool.wait_ge(sems["x2_out0"], at("x2_out0", B, 0))
                pool.wait_ge(sems["x2_out1"], at("x2_out1", B, 0))
                for k in range(BUFS):
                    gather(k)
                for k in range(BLOCKS):
                    pool.indirect_dma_start(b_f[:, k, :], None, t["b_f"], bass.IndirectOffsetOnAxis(expert_of[:, k:k + 1].bitcast(U32), 0),
                                            bounds_check=NT - 1, oob_is_err=False).then_inc(step["f_b"], 16)
                pool.wait_ge(step["f_b"], 16 * BLOCKS)

                def rstd(k):
                    pool.wait_ge(step["f_var_eps"], k + 1)
                    pool.tensor_tensor(r_f[:, k % 2, :], ve_f[:, k % 2, :], nhalf[:, 0:B], ALU.pow).then_inc(step["f_rstd"], 1)

                def scatter(k):
                    pool.wait_ge(step["f_sum"], B // 2 * (k + 1))
                    pool.indirect_dma_start(t["out"], bass.IndirectOffsetOnAxis(row_of[:, k:k + 1].bitcast(U32), 0), x_f[k % BUFS], None,
                                            bounds_check=S - 1, oob_is_err=False).then_inc(f_out[k % BUFS], 16)

                rstd(0)
                for m_ in range(PAIRS):
                    k, n = m_ // (B // 2), m_ % (B // 2)
                    pool.wait_ge(step["f_normed"], 2 * (m_ + 1))
                    rows = x_f[k % BUFS][:, 2 * n * E:2 * (n + 1) * E].rearrange("p (b e) -> p b e", e=E)
                    pool.tensor_tensor(rows, rows, b_f[:, k, :].rearrange("p (o e) -> p o e", o=1).broadcast_to([P, 2, E]), ALU.add).then_inc(step["f_biased"], 1)
                    if n == 1 and k:
                        scatter(k - 1)
                    if n == 3:
                        if k + 1 < BLOCKS:
                            rstd(k + 1)
                        if k and k - 1 + BUFS < BLOCKS:
                            pool.wait_ge(f_out[(k - 1) % BUFS], 16 * ((k - 1) // BUFS + 1))
                            gather(k - 1 + BUFS)
                scatter(BLOCKS - 1)


def _positions():
    div = np.exp(np.arange(0, PD, 2, dtype=np.float32) * np.float32(-np.log(10000.0) / PD))
    ang = np.arange(S, dtype=np.float32)[:, None] * div
    pe = np.zeros((S, PD), np.float32)
    pe[:, 0::2], pe[:, 1::2] = np.sin(ang), np.cos(ang)
    return pe


def _route_table():
    p, t_ = np.arange(P), np.arange(NT)
    rows = dict(slot=np.arange(P), first=NT - t_, seg_at=SEG * np.arange(S // SEG), seg=np.arange(SEGS), before=(t_[None, :] < t_[:, None]).reshape(-1),
                block_at=P * np.arange(1, BLOCKS), blk=np.arange(BLOCKS), blk_slot=(P * np.arange(BLOCKS)[None, :] + p[:, None]) // SEG,
                pos1=P * np.arange(C)[None, :] + p[:, None] + 1)
    return np.concatenate([np.broadcast_to(rows[k], (P, w)) for k, w in RT.items()], 1).astype(np.float32)


def _arrays(x, ctx_1024, mask_Bx1xSxS2_ik1, **w):
    def lay(a):
        return np.ascontiguousarray(np.asarray(a))

    n = {k[3:]: np.asarray(v) for k, v in w.items()}
    ip = n["attn_in_proj_w"]
    row, col = np.arange(P)[:, None], np.arange(P)[None, :]
    return dict(
        x=lay(np.asarray(x).reshape(B * S, E)),
        ctxT=lay(np.asarray(ctx_1024).transpose(0, 2, 1).reshape(B * E, S)),
        mask=lay(np.asarray(mask_Bx1xSxS2_ik1).reshape(B * S, S)),
        wz=lay(ip[:DI].T), wxbc=lay(ip[DI:DI + CT * P].T), wdt=lay(ip[DI + CT * P:].T),
        conv_w=lay(n["attn_conv_w"]), conv_b=lay(n["attn_conv_b"]), dt_bias=lay(n["attn_dt_bias"]),
        A_log=lay(n["attn_A_log"]), D=lay(n["attn_D"]), norm_w=lay(n["attn_norm_w"]),
        ln_w=lay(n["attn_ln_w"]), ln_b=lay(n["attn_ln_b"]), wout=lay(n["attn_out_proj_w"].T),
        adj=lay(n["xattn_adj"]), wq=lay(n["xattn_Wq"].T), wk=lay(n["xattn_Wk"].T), wv=lay(n["xattn_Wv"].T),
        wo=lay(n["xattn_Wo"].T), bq=lay(n["xattn_bq"]), bk=lay(n["xattn_bk"]), bv=lay(n["xattn_bv"]), bo=lay(n["xattn_bo"]),
        w_f=lay(n["ffn_W"].transpose(2, 0, 1)), b_f=lay(n["ffn_b"]), sigs=lay(n["ffn_tile_sigs"].T), pe=lay(_positions().T), rt=_route_table(),
        ident=np.eye(P, dtype=np.float32), triu=(row <= col).astype(np.float32), stril=(row > col).astype(np.float32),
    )


def kernel(**inputs):
    import concourse.bacc as bacc
    from concourse.bass_utils import run_bass_kernel_spmd

    nc = bacc.Bacc("TRN2", target_bir_lowering=False, num_devices=1)
    arrays = {f"in_{k}": v for k, v in _arrays(**inputs).items()}
    t = {k[3:]: nc.dram_tensor(k, v.shape, mybir.dt.from_np(v.dtype), kind="ExternalInput").ap() for k, v in arrays.items()}
    t["out"] = nc.dram_tensor("out", (S, ROW), F32, kind="ExternalOutput").ap()
    build(nc, t)
    r = run_bass_kernel_spmd(nc, [arrays], core_ids=[0])
    return np.ascontiguousarray(r.results[0]["out"].reshape(S, B, E).transpose(1, 0, 2))
```

```python
from contextlib import ExitStack

import numpy as np

import concourse.bass as bass
from concourse import mybir

F32 = mybir.dt.float32
F32R = mybir.dt.float32r
I32 = mybir.dt.int32
U32 = mybir.dt.uint32
ALU = mybir.AluOpType
ACT = mybir.ActivationFunctionType
AX = mybir.AxisListType

P = 128
B, S, E = 8, 512, 256
C = S // P
KE = E // P
DI, DS, NH, HD, DC = 512, 128, 8, 64, 4
KI = DI // P
CT = (DI + 2 * DS) // P
AH, AD = 16, 16
HG = 4
G = AH // HG
VW = 32
UG = HG * C
UNITS = G * UG
HS = 2
PRE = 3
RING = 4
LAG = 3
PV = UG + LAG
PROJ = UNITS + LAG + 3
EVAC_DVE = (1, 5, 7, 11, 15)
DRAIN = 15
SLOTS = UNITS + DRAIN
NT = 8
PD = 32
EPS = 1e-5
MASKED = -1e30
SEG = 32
SEGS = S // SEG + NT
BLOCKS = SEGS * SEG // P
PAIRS = BLOCKS * B // 2
BUFS = 5
ROW = B * E
RT = dict(slot=P, first=NT, seg_at=S // SEG, seg=SEGS, before=NT * NT, block_at=BLOCKS - 1, blk=BLOCKS, blk_slot=BLOCKS, pos1=C)


CONV_ORDER = (4, 5, 0, 1, 2, 3)
ON_POOL, ON_DVE = (4, 0, 2, 3), (5, 1)
HEAD = ("ln1", "ln2", "lnT", "dt1", "dt2", "bc", "conv", "cum")


MAIN = {
    ("k", 0): (0, {}), ("k", 1): (1, {}), ("ksplit",): (2, {"sp": 1}), ("v", 0): (2, {"dve": 1}), ("v", 1): (3, {"dve": 2, "sp": 1}),
    ("silu", 4): (1, {"dve": 1}), ("silu", 5): (2, {"dve": 1}), ("silu", 0): (3, {"dve": 2}), ("silu", 1): (4, {"dve": 1}),
    ("silu", 2): (5, {"dve": 1}), ("silu", 3): (6, {"dve": 1}), ("am", 0): (10, {}), ("am", 1): (12, {}), ("am", 2): (13, {}), ("am", 3): (16, {}),
    ("q1",): (50, {}), ("q2", 0): (51, {}), ("q2", 1): (52, {}), ("qsplit",): (53, {"sp": 1}),
}
CHUNK_AT = (7, 17, 27, 37)
CHUNK = {
    ("dmask",): (0, {}), ("seg", 0): (1, {}), ("seg", 1): (1, {}), ("gx",): (2, {"dve": 1, "pool": 1}), ("z",): (3, {"act": 1, "dve": 2}),
    ("w",): (4, {}), ("inter",): (5, {"dve": 1}), ("sdec",): (6, {}), ("intra",): (6, {"dve": 1}), ("state",): (7, {"dve": 2}), ("gate",): (8, {}),
    ("gate2",): (9, {}), ("o",): (9, {}), ("x1",): (10, {"dve": 1, "pool": 1}), ("xq",): (12, {}),
}
NEXT = {
    ("ln1",): (47, {}), ("ln2",): (54, {}), ("lnT",): (55, {"sp": 1}), ("dt1",): (58, {"dve": 1, "act": 2}), ("bc", 4): (60, {}),
    ("conv", 4): (61, {}), ("bc", 5): (62, {}), ("conv", 5): (64, {}), ("bc", 0): (64, {}), ("conv", 0): (65, {}), ("bc", 1): (65, {}),
    ("conv", 1): (67, {}), ("bc", 2): (69, {}), ("conv", 2): (69, {}), ("bc", 3): (70, {}), ("conv", 3): (71, {}), ("dt2", 0): (60, {}),
    ("dt2", 1): (62, {}), ("dt2", 2): (63, {}), ("dt2", 3): (64, {}), ("cum",): (71, {}),
}


def schedule():
    when = {e: [[] for _ in range(SLOTS)] for e in ("sp", "pe", "act", "dve", "pool")}

    def put(stage, slot, shift):
        for e in when:
            when[e][slot + shift.get(e, 0)].append(stage)

    for stage, (slot, shift) in MAIN.items():
        if stage[0] not in ("q1", "q2", "qsplit"):
            put(stage, slot, shift)
    for c in range(C):
        for stage, (slot, shift) in CHUNK.items():
            put(stage + (c,), CHUNK_AT[c] + slot, shift)
    for stage, (slot, shift) in MAIN.items():
        if stage[0] in ("q1", "q2", "qsplit"):
            put(stage, slot, shift)
    for stage, (slot, shift) in NEXT.items():
        put(stage, slot, shift)
    return when


WHEN = schedule()
M_TILES = []
for _head in (True, False):
    for _slot in WHEN["pe"]:
        for _s in _slot:
            if (_s[0] in HEAD) != _head:
                continue
            M_TILES += {
                "lnT": [("lnT", 0), ("lnT", 1)], "dt1": [("dt",)], "bc": [_s], "cum": [("cum",)], "z": [_s],
                "k": [_s], "v": [_s], "q1": [("xqT", 0), ("xqT", 1)], "q2": [("q",) + _s[1:]],
                "seg": [_s], "gx": [("gb",) + _s[1:], ("xt",) + _s[1:]],
                "inter": [_s] * (_s[-1] != 0), "intra": [_s], "state": [_s] * (_s[-1] != C - 1),
                "o": [("yT",) + _s[1:]], "x1": [("out",) + _s[1:]],
            }.get(_s[0], [])
M_BANKS = 3


def build(nc, t):
    ctx = ExitStack()
    with ctx:
        def sb(name, shape, dt=F32):
            return ctx.enter_context(nc.sbuf_tensor(name, shape, dt))

        def sem(name):
            return ctx.enter_context(nc.semaphore(name))

        qk_d = nc.dram_tensor("qk_d", (B, 2, 2, E, S), F32, kind="Internal").ap()
        x2_d = nc.dram_tensor("x2_d", (S, ROW), F32, kind="Internal").ap()

        ident = sb("ident", [P, P])
        triu = sb("triu", [P, P])
        stril = sb("stril", [P, P])
        ones = sb("ones", [P, P])
        nhalf = sb("nhalf", [P, 8])
        wxbc = sb("wxbc", [P, KE, CT * P])
        wz = sb("wz", [P, KE, DI])
        wdt = sb("wdt", [P, KE, NH])
        wout = sb("wout", [P, KI, E])
        wq, wk, wv, wo = (sb(n, [P, KE, E]) for n in ("wq", "wk", "wv", "wo"))
        lnw, lnb = sb("lnw", [P, KE]), sb("lnb", [P, KE])
        cw, cb = sb("cw", [P, CT, DC]), sb("cb", [P, CT])
        dtb, nega = sb("dtb", [P, C, NH]), sb("nega", [P, NH])
        alog = sb("alog", [P, NH])
        dsk = sb("dsk", [P, NH])
        nw = sb("nw", [P, KI])
        bq, bk = sb("bq", [P, KE]), sb("bk", [P, KE])
        bvb, bob = sb("bvb", [P, E]), sb("bob", [P, E])

        x_in = sb("x_in", [P, C, E])
        ctx_in = sb("ctx_in", [P, KE, S])
        st, mv, ve, rs = sb("st", [P, C, 6]), sb("mv", [P, C, 2]), sb("ve", [P, C, 2]), sb("rs", [P, C, 2])
        xn, xr = sb("xn", [P, C, E]), sb("xr", [P, C, E])
        x1, xq = sb("x1", [P, C, E]), xn
        xnT = sb("xnT", [P, KE, S])
        pre = sb("pre", [P, PRE, DC - 1 + S])
        xc = sb("xc", [P, CT, S])
        th = sb("th", [P, 2, S])
        zt, zs = sb("zt", [P, 2, DI]), sb("zs", [P, DI])
        dts = sb("dts", [P, 8, C, NH])
        dt, dA = sb("dt", [P, C, NH]), sb("dA", [P, C, NH])
        ecum = sb("ecum", [P, 2, C, NH])
        L = sb("L", [P, NH, P])
        dmask = L
        Gm, Bt = sb("Gm", [P, P]), sb("Bt", [P, DS])
        xt, xdt, xw = (sb(n, [P, NH, HD]) for n in ("xt", "xdt", "xw"))
        xD = xt
        ti, yg = sb("ti", [P, NH, HD]), sb("yg", [P, NH, HD])
        ygT = sb("ygT", [P, KI, P])
        tap = ygT
        state = sb("state", [P, NH, HD])
        sdec = state
        ss, se, rr = sb("ss", [P, 1]), sb("se", [P, 1]), sb("rr", [P, 1])
        st2, mv2, ve2, r2 = sb("st2", [P, 6]), sb("mv2", [P, 2]), sb("ve2", [P, 1]), sb("r2", [P, 1])
        x1b, xqT, kf = x1, xnT, zt
        kp = sb("kp", [P, 2, KE, S], F32R)
        qf = kf
        vm = sb("vm", [P, C, AH, VW])
        am_m = sb("am_m", [P, C, S])

        q_st = sb("q_st", [P, 2, HS, S], F32R)
        k_st = sb("k_st", [P, 2, HS, S], F32R)
        va = sb("va", [P, C, AH, VW])
        am = sb("am", [P, C, S])
        x1a = sb("x1a", [P, C, E])
        T = sb("T", [P, RING, S])
        nmx = sb("nmx", [P, RING])
        PT = sb("PT", [P, HG, C, S])
        OTs = sb("OTs", [P, S])
        rden = sb("rden", [P, C, HG])
        On = sb("On", [P, C, AH, AD])
        OnT = OTs[:, :].rearrange("p (b k i) -> p b k i", b=2, k=KE)

        rt = sb("rt", [P, sum(RT.values())])
        row_of, expert_of = sb("row_of", [P, BLOCKS], I32), sb("expert_of", [P, BLOCKS], I32)
        seg_expert = sb("seg_expert", [1, SEGS], I32)
        flat = PT[:, :, :, :].rearrange("p h k s -> p (h k s)")
        w_f = flat[:, 0:KE * NT * E].rearrange("p (k t e) -> p k t e", k=KE, t=NT)
        x_f = [flat[:, KE * NT * E:KE * NT * E + ROW], flat[:, KE * NT * E + ROW:KE * NT * E + 2 * ROW],
               xc[:, :, :].rearrange("p c s -> p (c s)")[:, 0:ROW], va[:, :, :, :].rearrange("p c h v -> p (c h v)"),
               T[:, :, :].rearrange("p r s -> p (r s)")]
        seg_w = [ap[:, :, :].rearrange("p c s -> p (c s)").rearrange("p (j k e) -> p j k e", j=P // SEG, k=KE) for ap in (am_m, am)]
        b_f = vm[:, :, :, :].rearrange("p c h v -> p (c h v)")[:, 0:BLOCKS * E].rearrange("p (k e) -> p k e", e=E)
        n_f, t_f = zt, xnT
        small = ti[:, :, :].rearrange("p h d -> p (h d)").rearrange("p (b n) -> p b n", b=2)
        st_f, mv_f = small[:, :, 0:6 * B], small[:, :, 6 * B:8 * B]
        ve_f, r_f = small[:, :, 8 * B:9 * B], small[:, :, 9 * B:10 * B]

        pm = [ctx.enter_context(nc.psum_tensor(f"pm{i}", [P, 512], F32)) for i in range(M_BANKS)]
        ps = [ctx.enter_context(nc.psum_tensor(f"ps{i}", [P, 512], F32)) for i in range(2)]
        pt = [ctx.enter_context(nc.psum_tensor(f"pt{i}", [P, 512], F32)) for i in range(2)]
        po = ctx.enter_context(nc.psum_tensor("po", [P, 512], F32))

        consts, more_consts = sem("consts"), sem("more_consts")
        bank_fills = [sum(1 for i in range(len(M_TILES)) if i % M_BANKS == k) for k in range(M_BANKS)]
        m_full = [sem(f"m_full{k}") for k in range(M_BANKS)]
        m_read = [sem(f"m_read{k}") for k in range(M_BANKS)]
        setup = {n: sem(f"setup_{n}") for n in ("act", "dve", "ready", "scaled")}
        PER = dict(
            x_loaded=16, ctx_loaded=16, mask_loaded=16, stats=C, mean_var=C, var_eps=2, rstd=1, normed=C, ln_x=C, residual=1,
            conv_pool=4 * DC, tap_product=4 * (DC - 1), conv_dve=2 * DC, tanh=CT, silu=CT, z_tanh=C, dt_step=12, dt_exp=1, dt_series=2, dt_ready=2, gram_masked=C, decay_mask=C, L=2 * C,
            weights=C, x_dt=C, x_decayed=C - 1, x_D=C, y_inter=C - 1, y_gated=C, sumsq=C, meansq=C, gate_rstd=C, state_decayed=C - 2,
            stats2=C, mean_var2=C, var_eps2=C, rstd2=C, query_normed=C, x1_bias=C, k_high=2, k_low=2, q_high=2, q_low=2,
            v_half=2, mask_bias=C, score_bias=16, qk_out=16 * 8,
            va_moved=16, x1a_moved=16, bias_moved01=16, bias_moved23=16,
            st_in0=16 * 8 * 4, st_in1=16 * 8 * 4, score=UNITS, row_max=UNITS, probs=UNITS, turned=UNITS, evac_act=G * (UG - len(EVAC_DVE)), evac_dve=G * len(EVAC_DVE),
            pv=G, sums_out=G, sums_turned=G, recip=G, heads_normed=G, heads_turned=C, heads_copied=C, projected=C, x2_rows=C,
            x2_out0=16 * 2, x2_out1=16 * 2)
        sems = {n: sem(n) for n in PER}

        def at(name, b, k):
            v = b * PER[name] + k
            return max(v, 0) if isinstance(v, int) else v

        def alone(eng, sem, v):
            if not isinstance(v, int):
                v = eng.to_reg(v)
                eng.wait_ge(consts, CONSTS)
            return sem, v

        def tile(name):
            i = M_TILES.index(name)
            return i % M_BANKS, i // M_BANKS + 1

        def bank(name):
            return pm[tile(name)[0]]

        def full(name):
            return m_full[tile(name)[0]]

        def read(name):
            return m_read[tile(name)[0]]

        def full_at(name, b):
            v = b * bank_fills[tile(name)[0]] + tile(name)[1]
            return max(v, 0) if isinstance(v, int) else v

        def read_at(name, b):
            return full_at(name, b)

        def free_at(name, b):
            return b * bank_fills[tile(name)[0]] + tile(name)[1] - 1

        step = {n: sem(n) for n in (
            "f_signs", "f_scores", "f_routed", "f_counts", "f_onehot", "f_slots", "f_tables", "f_rows", "f_w", "f_placed", "f_b",
            "f_stats", "f_mean_var", "f_var_eps", "f_rstd", "f_normed", "f_turned", "f_copied", "f_product", "f_sum", "f_biased")}
        f_in = [sem(f"f_in{i}") for i in range(BUFS)]
        f_out = [sem(f"f_out{i}") for i in range(BUFS)]
        route_loads = sem("route_loads")
        rcol, _n = {}, 0
        for _k, _w in RT.items():
            rcol[_k] = rt[:, _n:_n + _w]
            _n += _w
        tmp = PT[:, :, :, :].rearrange("p h k s -> p (h k s)")
        pos_e, sig_e = tmp[0:PD, 0:S], tmp[0:PD, S:S + NT]
        LEFT, RIGHT, OH, ST = 1024, 2048, 2600, 2700

        def column(ap, n):
            return ap[:, :], t[n].rearrange("(k p) -> p k", p=P)

        def matrix(ap, n):
            return ap[:, :, :], t[n].rearrange("(k p) n -> p k n", p=P)

        def row(ap, n):
            return ap, t[n].partition_broadcast(P)

        loads = [(ident[:, :], t["ident"]), (triu[:, :], t["triu"]), matrix(wxbc, "wxbc"), matrix(wdt, "wdt"), column(lnw, "ln_w"),
                 column(lnb, "ln_b"), (cw[:, :, :], t["conv_w"].rearrange("(k p) j -> p k j", p=P)), column(cb, "conv_b"),
                 row(alog[:, :], "A_log")] + [row(dtb[:, c, :], "dt_bias") for c in range(C)]
        more_loads = [matrix(wk, "wk"), matrix(wv, "wv"), (stril[:, :], t["stril"]), matrix(wz, "wz"), matrix(wout, "wout"), matrix(wq, "wq"),
                      matrix(wo, "wo"), row(dsk[:, :], "D"), column(nw, "norm_w"), column(bq, "bq"), column(bk, "bk"),
                      row(bvb[:, :], "bv"), row(bob[:, :], "bo")]
        CONSTS, MORE = 16 * len(loads), 16 * len(more_loads)

        def batches(eng, body, peeled=0, between=None):
            body(None, None, 0)
            if between:
                between()
            body(0, None, 1)
            body(1, 0, 2)
            with eng.Fori(1, B - 2 - peeled) as a:
                body(a + 1, a, a + 2)
            for a in range(B - 2 - peeled, B - 2):
                body(a + 1, a, a + 2)
            body(B - 1, B - 2, None)
            body(None, B - 1, None)

        def unit(u):
            w = u % UG
            return u // UG, w % C, w // C

        def evac_by(u):
            return "evac_dve" if u % UG in EVAC_DVE else "evac_act"

        def evac_at(u):
            return u // UG * (len(EVAC_DVE) if u % UG in EVAC_DVE else UG - len(EVAC_DVE)) + sum(1 for w in range(u % UG + 1) if (w in EVAC_DVE) == (u % UG in EVAC_DVE))

        def mt_order(mt):
            return CONV_ORDER.index(mt)

        def conv_by(mt):
            return "conv_pool" if mt in ON_POOL else "conv_dve"

        def taps_at(mt, taps):
            return DC * (ON_POOL if mt in ON_POOL else ON_DVE).index(mt) + taps

        with nc.allow_non_contiguous_dma("vectors of weights, once"), nc.Block() as block:

            @block.sync
            def _(sp):
                def load_x(b):
                    sp.dma_start(x_in[:, :, :], t["x"][bass.ds(b * S, S), :].rearrange("(c p) e -> p c e", p=P)).then_inc(sems["x_loaded"], 16)

                def load_ctx(b):
                    sp.dma_start(ctx_in[:, :, :], t["ctxT"][bass.ds(b * E, E), :].rearrange("(k p) s -> p k s", p=P)).then_inc(sems["ctx_loaded"], 16)

                def load_mask(b):
                    sp.dma_start(am_m[:, :, :].bitcast(I32), t["mask"][bass.ds(b * S, S), :].rearrange("(c p) s -> p c s", p=P)).then_inc(sems["mask_loaded"], 16)

                def out_parts(b, which, parts):
                    for hl in range(2):
                        for k in range(KE):
                            sp.dma_start(qk_d[bass.ds(b, 1), which, hl, k * P:(k + 1) * P, :].rearrange("o p s -> p (o s)"),
                                         parts[:, hl, k, :].bitcast(F32)).then_inc(sems["qk_out"], 16)

                def stage(a, n):
                    for which, st_, order in ((0, q_st, (0, 0, 1, 1)), (1, k_st, (0, 1, 0, 1))):
                        for r, hl in enumerate(order):
                            src = qk_d[bass.ds(a, 1), which, hl, n * HS * AD:(n + 1) * HS * AD, :]
                            sp.dma_start(st_[r * AD:(r + 1) * AD, n % 2, :, :].bitcast(F32),
                                         src.rearrange("o (h d) s -> d (o h) s", d=AD)).then_inc(sems[f"st_in{n % 2}"], 16)

                load_x(0)
                for dst, src in loads:
                    sp.dma_start(dst, src).then_inc(consts, 16)
                load_ctx(0)
                load_mask(0)
                sp.dma_start(pos_e, t["pe"]).then_inc(route_loads, 16)
                sp.dma_start(sig_e, t["sigs"]).then_inc(route_loads, 16)
                sp.dma_start(rt[:, :], t["rt"]).then_inc(route_loads, 16)

                def body(b, a, nxt):
                    for u in range(SLOTS):
                        if b is not None and u == 0 and not (isinstance(b, int) and b == 0):
                            sp.wait_ge(*alone(sp, sems["bias_moved01"], at("bias_moved01", b, 0)))
                            sp.wait_ge(*alone(sp, sems["bias_moved23"], at("bias_moved23", b, 0)))
                            load_mask(b)
                        if a is not None:
                            if u and u % (HS * C) == 0 and u // (HS * C) + 1 < AH // HS:
                                n = u // (HS * C) + 1
                                sp.wait_ge(*alone(sp, sems["score"], at("score", a, HS * C * (n - 1))))
                                stage(a, n)
                            if PROJ + 1 <= u < PROJ + 1 + C:
                                q = u - PROJ - 1
                                sp.wait_ge(*alone(sp, sems["x2_rows"], at("x2_rows", a, q + 1)))
                                sp.dma_start(x2_d[q * P:(q + 1) * P, bass.ds(a * E, E)], x1a[:, q, :]).then_inc(sems[f"x2_out{q % 2}"], 16)
                        for stg in WHEN["sp"][u]:
                            if stg == ("lnT",) and nxt is not None and not (isinstance(nxt, int) and nxt == B - 1):
                                sp.wait_ge(*alone(sp, sems["normed"], at("normed", nxt, C)))
                                sp.wait_ge(*alone(sp, sems["residual"], at("residual", nxt, 1)))
                                load_x(nxt + 1)
                            if stg == ("ksplit",) and b is not None:
                                sp.wait_ge(*alone(sp, sems["k_low"], at("k_low", b, 2)))
                                sp.wait_ge(*alone(sp, sems["k_high"], at("k_high", b, 2)))
                                out_parts(b, 1, kp)
                            if stg == ("v", 1) and nxt is not None and b is not None:
                                sp.wait_ge(*alone(sp, full(("v", 1)), full_at(("v", 1), b)))
                                load_ctx(b + 1)
                            if stg == ("qsplit",) and b is not None:
                                sp.wait_ge(*alone(sp, sems["q_low"], at("q_low", b, 2)))
                                sp.wait_ge(*alone(sp, sems["q_high"], at("q_high", b, 2)))
                                out_parts(b, 0, kp)
                        if b is not None:
                            if u == UNITS - HS * C + 1:
                                sp.wait_ge(*alone(sp, sems["qk_out"], at("qk_out", b, 16 * 8)))
                                sp.wait_ge(*alone(sp, sems["score"], at("score", b, -HS * C)))
                                if isinstance(b, int) and b == 0:
                                    sp.wait_ge(setup["dve"], 8)
                                stage(b, 0)
                            if u == UNITS:
                                sp.wait_ge(*alone(sp, sems["score_bias"], at("score_bias", b, 16)))
                                sp.wait_ge(*alone(sp, sems["row_max"], at("row_max", b, 0)))
                                sp.dma_start(am[:, 0:2, :], am_m[:, 0:2, :]).then_inc(sems["bias_moved01"], 16)
                                sp.dma_start(am[:, 2:4, :], am_m[:, 2:4, :]).then_inc(sems["bias_moved23"], 16)
                                sp.wait_ge(*alone(sp, sems["score"], at("score", b, 0)))
                                stage(b, 1)
                            if u == UNITS + LAG + 1:
                                sp.wait_ge(*alone(sp, sems["v_half"], at("v_half", b, 2)))
                                sp.wait_ge(*alone(sp, read(("v", 0)), read_at(("v", 0), b)))
                                sp.wait_ge(*alone(sp, read(("v", 1)), read_at(("v", 1), b)))
                                sp.wait_ge(*alone(sp, sems["pv"], at("pv", b, 0)))
                                sp.dma_start(va[:, :, :, :], vm[:, :, :, :]).then_inc(sems["va_moved"], 16)
                            if u == SLOTS - 1:
                                sp.wait_ge(*alone(sp, sems["x1_bias"], at("x1_bias", b, C)))
                                sp.wait_ge(*alone(sp, sems["x2_out0"], at("x2_out0", b, 0)))
                                sp.wait_ge(*alone(sp, sems["x2_out1"], at("x2_out1", b, 0)))
                                sp.dma_start(x1a[:, :, :], x1b[:, :, :]).then_inc(sems["x1a_moved"], 16)

                batches(sp, body, peeled=1)
                sp.wait_ge(sems["pv"], at("pv", B, 0))
                sp.dma_start(w_f, t["w_f"].rearrange("(k p) t e -> p k t e", p=P)).then_inc(step["f_w"], 16)
                for i in range(BUFS):
                    sp.wait_ge(f_out[i], 16 * len(range(i, BLOCKS, BUFS)))

            @block.tensor
            def _(pe):
                pe.wait_ge(consts, CONSTS)
                pe.wait_ge(setup["ready"], 3)

                def mm(out, lhsT, rhs, first, last):
                    return pe.matmul(out, lhsT, rhs, start=first, stop=last)

                def m(stg, b):
                    k = stg[0]
                    if k == "lnT":
                        pe.wait_ge(sems["normed"], at("normed", b, C))
                        for kt in range(KE):
                            pe.wait_ge(read(("lnT", kt)), free_at(("lnT", kt), b))
                            for c in range(C):
                                ins = pe.transpose(bank(("lnT", kt))[:, c * P:(c + 1) * P], xn[:, c, kt * P:(kt + 1) * P], ident[:, :])
                            ins.then_inc(full(("lnT", kt)), 1)
                    if k == "dt1":
                        pe.wait_ge(read(("dt",)), free_at(("dt",), b))
                        for kt in range(KE):
                            pe.wait_ge(read(("lnT", kt)), read_at(("lnT", kt), b))
                        for c in range(C):
                            for kt in range(KE):
                                ins = mm(bank(("dt",))[:, c * NH:(c + 1) * NH], xnT[:, kt, c * P:(c + 1) * P], wdt[:, kt, :], kt == 0, kt == KE - 1)
                        ins.then_inc(full(("dt",)), 1)
                    if k == "bc":
                        pe.wait_ge(read(stg), free_at(stg, b))
                        for kt in range(KE):
                            ins = mm(bank(stg)[:, :], wxbc[:, kt, stg[1] * P:(stg[1] + 1) * P], xnT[:, kt, :], kt == 0, kt == KE - 1)
                        ins.then_inc(full(stg), 1)
                    if k == "z":
                        pe.wait_ge(read(stg), free_at(stg, b))
                        for kt in range(KE):
                            ins = mm(bank(stg)[:, :], xnT[:, kt, stg[1] * P:(stg[1] + 1) * P], wz[:, kt, :], kt == 0, kt == KE - 1)
                        ins.then_inc(full(stg), 1)
                    if k == "cum":
                        pe.wait_ge(read(("cum",)), free_at(("cum",), b))
                        pe.wait_ge(sems["dt_ready"], at("dt_ready", b, 2))
                        mm(bank(("cum",))[:, 0:C * NH], triu[:, :], dA[:, :, :].rearrange("p c h -> p (c h)"), True, True)
                        mm(bank(("cum",))[:, C * NH:2 * C * NH], ones[:, :], dA[:, :, :].rearrange("p c h -> p (c h)"), True, True).then_inc(full(("cum",)), 1)
                    if k == "k":
                        pe.wait_ge(sems["ctx_loaded"], at("ctx_loaded", b, 16))
                        ct = stg[1]
                        pe.wait_ge(read(("k", ct)), free_at(("k", ct), b))
                        for kt in range(KE):
                            ins = mm(bank(("k", ct))[:, :], wk[:, kt, ct * P:(ct + 1) * P], ctx_in[:, kt, :], kt == 0, kt == KE - 1)
                        ins.then_inc(full(("k", ct)), 1)
                    if k == "v":
                        j = stg[1]
                        pe.wait_ge(read(("v", j)), free_at(("v", j), b))
                        for c in (2 * j, 2 * j + 1):
                            for kt in range(KE):
                                ins = mm(bank(("v", j))[:, (c % 2) * E:(c % 2 + 1) * E], ctx_in[:, kt, c * P:(c + 1) * P], wv[:, kt, :], kt == 0, kt == KE - 1)
                        ins.then_inc(full(("v", j)), 1)
                    if k == "seg":
                        c = stg[2]
                        pe.wait_ge(sems["decay_mask"], at("decay_mask", b, c + 1))
                        j = stg[1]
                        pe.wait_ge(read(("seg", j, c)), free_at(("seg", j, c), b))
                        mm(bank(("seg", j, c))[:, :], stril[:, :], dmask[:, 4 * j:4 * j + 4, :].rearrange("p h i -> p (h i)"), True, True).then_inc(full(("seg", j, c)), 1)
                    if k == "gx":
                        c = stg[1]
                        cs = slice(c * P, (c + 1) * P)
                        pe.wait_ge(sems["silu"], at("silu", b, CT))
                        pe.wait_ge(read(("gb", c)), free_at(("gb", c), b))
                        mm(bank(("gb", c))[:, 0:P], xc[:, 4, cs], xc[:, 5, cs], True, True)
                        pe.transpose(bank(("gb", c))[:, P:2 * P], xc[:, 4, cs], ident[:, :]).then_inc(full(("gb", c)), 1)
                        pe.wait_ge(read(("xt", c)), free_at(("xt", c), b))
                        for kt in range(KI):
                            ins = pe.transpose(bank(("xt", c))[:, kt * P:(kt + 1) * P], xc[:, kt, cs], ident[:, :])
                        ins.then_inc(full(("xt", c)), 1)
                    if k == "inter":
                        c = stg[1]
                        if c:
                            pe.wait_ge(read(("inter", c)), free_at(("inter", c), b))
                            pe.wait_ge(read(("state", c - 1)), read_at(("state", c - 1), b))
                            mm(bank(("inter", c))[:, :], xc[:, 5, c * P:(c + 1) * P], state[:, :, :].rearrange("p h d -> p (h d)"), True, True).then_inc(full(("inter", c)), 1)
                    if k == "intra":
                        c = stg[1]
                        pe.wait_ge(read(("intra", c)), free_at(("intra", c), b))
                        pe.wait_ge(sems["weights"], at("weights", b, c + 1))
                        pe.wait_ge(sems["x_dt"], at("x_dt", b, c + 1))
                        for h in range(NH):
                            ins = mm(bank(("intra", c))[:, h * HD:(h + 1) * HD], L[:, h, :], xdt[:, h, :], True, True)
                        ins.then_inc(full(("intra", c)), 1)
                    if k == "state":
                        c = stg[1]
                        if c < C - 1:
                            pe.wait_ge(read(("state", c)), free_at(("state", c), b))
                            pe.wait_ge(sems["x_decayed"], at("x_decayed", b, c + 1))
                            mm(bank(("state", c))[:, :], Bt[:, :], xw[:, :, :].rearrange("p h d -> p (h d)"), True, True).then_inc(full(("state", c)), 1)
                    if k == "o":
                        c = stg[1]
                        pe.wait_ge(read(("yT", c)), free_at(("yT", c), b))
                        pe.wait_ge(sems["y_gated"], at("y_gated", b, c + 1))
                        for kt in range(KI):
                            ins = pe.transpose(bank(("yT", c))[:, kt * P:(kt + 1) * P], yg[:, :, :].rearrange("p h d -> p (h d)")[:, kt * P:(kt + 1) * P], ident[:, :])
                        ins.then_inc(full(("yT", c)), 1)
                    if k == "x1":
                        c = stg[1]
                        pe.wait_ge(read(("out", c)), free_at(("out", c), b))
                        pe.wait_ge(read(("yT", c)), read_at(("yT", c), b))
                        for kt in range(KI):
                            ins = mm(bank(("out", c))[:, 0:E], ygT[:, kt, :], wout[:, kt, :], kt == 0, kt == KI - 1)
                        ins.then_inc(full(("out", c)), 1)
                    if k == "q1":
                        pe.wait_ge(sems["query_normed"], at("query_normed", b, C))
                        for kt in range(KE):
                            pe.wait_ge(read(("xqT", kt)), free_at(("xqT", kt), b))
                            for c in range(C):
                                ins = pe.transpose(bank(("xqT", kt))[:, c * P:(c + 1) * P], xq[:, c, kt * P:(kt + 1) * P], ident[:, :])
                            ins.then_inc(full(("xqT", kt)), 1)
                    if k == "q2":
                        for kt in range(KE):
                            pe.wait_ge(read(("xqT", kt)), read_at(("xqT", kt), b))
                        ct = stg[1]
                        pe.wait_ge(read(("q", ct)), free_at(("q", ct), b))
                        for kt in range(KE):
                            ins = mm(bank(("q", ct))[:, :], wq[:, kt, ct * P:(ct + 1) * P], xqT[:, kt, :], kt == 0, kt == KE - 1)
                        ins.then_inc(full(("q", ct)), 1)

                def score(a, u):
                    g, qt, hh = unit(u)
                    n, hs = u // (HS * C), u // C % HS
                    if u % (HS * C) == 0:
                        pe.wait_ge(sems[f"st_in{n % 2}"], at(f"st_in{n % 2}", a, 16 * 8 * (n // 2 + 1)))
                    pe.wait_ge(sems["row_max"], at("row_max", a, u - 1))
                    mm(ps[u % 2][:, :], q_st[:, n % 2, hs, qt * P:(qt + 1) * P], k_st[:, n % 2, hs, :], True, True).then_inc(sems["score"], 1)

                def turn(a, u):
                    pe.wait_ge(sems["probs"], at("probs", a, u + 1))
                    if u < 2:
                        pe.wait_ge(sems["x2_rows"], at("x2_rows", a, 0))
                    pe.wait_ge(sems[evac_by(u - 2)], at(evac_by(u - 2), a, evac_at(u - 2)))
                    for kt in range(C):
                        ins = pe.transpose(pt[u % 2][:, kt * P:(kt + 1) * P], T[:, u % RING, kt * P:(kt + 1) * P], ident[:, :])
                    ins.then_inc(sems["turned"], 1)

                def pv(a, g):
                    if g == 0:
                        pe.wait_ge(sems["va_moved"], at("va_moved", a, 16))
                    pe.wait_ge(sems[evac_by(UG * g + UG - 2)], at(evac_by(UG * g + UG - 2), a, evac_at(UG * g + UG - 2)))
                    pe.wait_ge(sems[evac_by(UG * g + UG - 1)], at(evac_by(UG * g + UG - 1), a, evac_at(UG * g + UG - 1)))
                    pe.wait_ge(sems["heads_normed"], at("heads_normed", a, g))
                    for kt in range(C):
                        for hh in range(HG):
                            ins = pe.matmul(po[VW * hh:VW * (hh + 1), :], va[:, kt, g * HG + hh, :], PT[:, hh, kt, :],
                                            start=(kt == 0), stop=(kt == C - 1), tile_position=(0, VW * hh), skip_group_check=True)
                    ins.then_inc(sems["pv"], 1)

                def turn_out(a, g):
                    pe.wait_ge(sems["sums_out"], at("sums_out", a, g + 1))
                    for q in range(C):
                        ins = pe.transpose(po[:, q * P:(q + 1) * P], OTs[:, q * P:(q + 1) * P], ident[:, :])
                    ins.then_inc(sems["sums_turned"], 1)

                def project_turn(a, q):
                    if q == 0:
                        pe.wait_ge(sems["heads_normed"], at("heads_normed", a, G))
                    for kt in range(KE):
                        ins = pe.transpose(ps[q % 2][:, kt * P:(kt + 1) * P], On[:, q, :, :].rearrange("p h d -> p (h d)")[:, kt * P:(kt + 1) * P], ident[:, :])
                    ins.then_inc(sems["heads_turned"], 1)

                def project(a, q):
                    pe.wait_ge(sems["heads_copied"], at("heads_copied", a, q + 1))
                    if q >= 2:
                        pe.wait_ge(sems["x2_rows"], at("x2_rows", a, q - 1))
                    for kt in range(KE):
                        ins = mm(pt[q % 2][:, 0:E], OnT[:, q % 2, kt, :], wo[:, kt, :], kt == 0, kt == KE - 1)
                    ins.then_inc(sems["projected"], 1)

                def body(b, a, nxt):
                    for u in range(SLOTS):
                        if a is not None:
                            if u < UNITS:
                                score(a, u)
                            if LAG <= u < UNITS + LAG:
                                turn(a, u - LAG)
                            if u >= PV and (u - PV) % UG == 0 and (u - PV) // UG < G:
                                pv(a, (u - PV) // UG)
                            if u >= PV + 1 and (u - PV - 1) % UG == 0 and (u - PV - 1) // UG < G:
                                turn_out(a, (u - PV - 1) // UG)
                            if PROJ <= u < PROJ + C:
                                project_turn(a, u - PROJ)
                            if PROJ + 1 <= u < PROJ + 1 + C:
                                project(a, u - PROJ - 1)
                        for stg in WHEN["pe"][u]:
                            mb = nxt if stg[0] in HEAD else b
                            if mb is not None:
                                m(stg, mb)

                def between():
                    pe.wait_ge(step["f_signs"], 1)
                    for c in range(C):
                        ins = pe.matmul(po[:, c * NT:(c + 1) * NT], pos_e[:, c * P:(c + 1) * P], sig_e, start=True, stop=True)
                    ins.then_inc(step["f_scores"], 1)
                    pe.wait_ge(step["f_onehot"], 1)
                    oh = tmp[:, OH:OH + C * NT]
                    for c in range(C):
                        for k in range(c + 1):
                            pe.matmul(po[:, c * NT:(c + 1) * NT], triu[:, :] if k == c else ones[:, :], oh[:, k * NT:(k + 1) * NT], start=(k == 0), stop=(k == c))
                    for c in range(C):
                        ins = pe.matmul(po[:, C * NT:(C + 1) * NT], ones[:, :], oh[:, c * NT:(c + 1) * NT], start=(c == 0), stop=(c == C - 1))
                    ins.then_inc(step["f_counts"], 1)
                    pe.wait_ge(step["f_tables"], 1)
                    for c in range(C):
                        ins = pe.matmul(po[:, 0:BLOCKS], tmp[:, LEFT + c * P:LEFT + (c + 1) * P], tmp[:, RIGHT + c * BLOCKS:RIGHT + (c + 1) * BLOCKS],
                                        start=(c == 0), stop=(c == C - 1))
                    ins.then_inc(step["f_slots"], 1)
                    pe.wait_ge(more_consts, MORE)
                    pe.wait_ge(setup["scaled"], 1 + KI)

                batches(pe, body, between=between)

                for m_ in range(PAIRS + 1):
                    if m_ < PAIRS:
                        pe.wait_ge(step["f_normed"], 2 * (m_ + 1))
                        pe.wait_ge(step["f_copied"], max(0, m_ - 1))
                        for q in range(2 * KE):
                            ins = pe.transpose(pt[m_ % 2][:, q * P:(q + 1) * P], n_f[:, m_ % 2, q * P:(q + 1) * P], ident[:, :])
                        ins.then_inc(step["f_turned"], 1)
                    if m_:
                        w = m_ - 1
                        pe.wait_ge(step["f_placed"], P // SEG * (w // (B // 2) + 1))
                        pe.wait_ge(step["f_copied"], w + 1)
                        pe.wait_ge(step["f_sum"], max(0, w - 1))
                        for h in range(2):
                            for kt in range(KE):
                                for j in range(P // SEG):
                                    ins = pe.matmul(ps[w % 2][SEG * j:SEG * (j + 1), h * E:(h + 1) * E],
                                                    t_f[:, w % 2, (h * KE + kt) * P + SEG * j:(h * KE + kt) * P + SEG * (j + 1)],
                                                    seg_w[w // (B // 2) % 2][:, j, kt, :],
                                                    start=(kt == 0), stop=(kt == KE - 1), tile_position=(0, SEG * j), skip_group_check=True)
                        ins.then_inc(step["f_product"], 1)

            @block.scalar
            def _(act):
                for dst, src in more_loads:
                    act.dma_start(dst, src).then_inc(more_consts, 16)
                act.wait_ge(consts, CONSTS)
                act.activation(nega[:, :], alog[:, :], ACT.Exp).then_inc(setup["act"], 1)
                act.wait_ge(setup["act"], 1)
                act.mul(nega[:, :], nega[:, :], -1.0).then_inc(setup["ready"], 1)
                act.wait_ge(setup["ready"], 3)

                def m(stg, b):
                    k = stg[0]
                    if k == "lnT":
                        for kt in range(KE):
                            act.wait_ge(full(("lnT", kt)), full_at(("lnT", kt), b))
                            act.activation(xnT[:, kt, :], bank(("lnT", kt))[:, :], ACT.Identity, bias=lnb[:, kt:kt + 1], scale=lnw[:, kt:kt + 1]).then_inc(read(("lnT", kt)), 1)
                    if k == "dt1":
                        act.wait_ge(sems["dt_step"], at("dt_step", b, 2))
                        act.activation(dts[:, 2, :, :], dts[:, 1, :, :], ACT.Exp, scale=-1.0).then_inc(sems["dt_exp"], 1)
                    if k == "bc":
                        act.wait_ge(full(stg), full_at(stg, b))
                        i = mt_order(stg[1])
                        if i >= PRE:
                            act.wait_ge(sems[conv_by(CONV_ORDER[i - PRE])], at(conv_by(CONV_ORDER[i - PRE]), b, taps_at(CONV_ORDER[i - PRE], DC)))
                        else:
                            act.wait_ge(sems[conv_by(CONV_ORDER[i - PRE])], at(conv_by(CONV_ORDER[i - PRE]), b - 1, taps_at(CONV_ORDER[i - PRE], DC)))
                        act.copy(pre[:, i % PRE, DC - 1:], bank(stg)[:, :]).then_inc(read(stg), 1)
                    if k == "z":
                        act.wait_ge(full(stg), full_at(stg, b))
                        if stg[1] == 0:
                            act.wait_ge(sems["k_low"], at("k_low", b, 2))
                        if stg[1] >= 2:
                            act.wait_ge(read(("z", stg[1] - 2)), read_at(("z", stg[1] - 2), b))
                        act.activation(zt[:, stg[1] % 2, :], bank(stg)[:, :], ACT.Tanh, scale=0.5).then_inc(sems["z_tanh"], 1)
                    if k == "cum":
                        act.wait_ge(full(("cum",)), full_at(("cum",), b))
                        act.activation(ecum[:, :, :, :].rearrange("p a c h -> p (a c h)"), bank(("cum",))[:, 0:2 * C * NH], ACT.Exp).then_inc(read(("cum",)), 1)
                    if k == "k":
                        act.wait_ge(sems["q_low"], at("q_low", b, 0))
                        ct = stg[1]
                        act.wait_ge(full(("k", ct)), full_at(("k", ct), b))
                        act.activation(kf[:, ct, :], bank(("k", ct))[:, :], ACT.Identity, bias=bk[:, ct:ct + 1]).then_inc(read(("k", ct)), 1)
                    if k == "seg":
                        c = stg[2]
                        if c:
                            act.wait_ge(full(("intra", c - 1)), full_at(("intra", c - 1), b))
                        else:
                            act.wait_ge(full(("intra", C - 1)), full_at(("intra", C - 1), b - 1))
                        j = stg[1]
                        act.wait_ge(full(("seg", j, c)), full_at(("seg", j, c), b))
                        act.activation(L[:, 4 * j:4 * j + 4, :].rearrange("p h i -> p (h i)"), bank(("seg", j, c))[:, :], ACT.Exp).then_inc(read(("seg", j, c)), 1)
                    if k == "gx":
                        c = stg[1]
                        act.wait_ge(full(("xt", c)), full_at(("xt", c), b))
                        if c:
                            act.wait_ge(read(("intra", c - 1)), read_at(("intra", c - 1), b))
                        act.copy(xt[:, :, :].rearrange("p h d -> p (h d)"), bank(("xt", c))[:, :]).then_inc(read(("xt", c)), 1)
                    if k == "gate":
                        c = stg[1]
                        act.wait_ge(sems["y_gated"], at("y_gated", b, c + 1))
                        act.activation(th[:, 0, :], yg[:, :, :].rearrange("p h d -> p (h d)"), ACT.Square, accum_out=ss[:, :]).then_inc(sems["sumsq"], 1)
                    if k == "o":
                        c = stg[1]
                        act.wait_ge(full(("yT", c)), full_at(("yT", c), b))
                        act.copy(ygT[:, :, :].rearrange("p k i -> p (k i)"), bank(("yT", c))[:, :]).then_inc(read(("yT", c)), 1)
                    if k == "silu":
                        silu(b, stg[1])
                    if k == "q1":
                        for kt in range(KE):
                            act.wait_ge(full(("xqT", kt)), full_at(("xqT", kt), b))
                            act.copy(xqT[:, kt, :], bank(("xqT", kt))[:, :]).then_inc(read(("xqT", kt)), 1)
                    if k == "q2":
                        act.wait_ge(sems["k_low"], at("k_low", b, 2))
                        ct = stg[1]
                        act.wait_ge(full(("q", ct)), full_at(("q", ct), b))
                        act.activation(qf[:, ct, :], bank(("q", ct))[:, :], ACT.Identity, bias=bq[:, ct:ct + 1], scale=AD ** -0.5).then_inc(read(("q", ct)), 1)

                def silu(b, mt):
                    act.wait_ge(sems[conv_by(mt)], at(conv_by(mt), b, taps_at(mt, DC)))
                    act.wait_ge(sems["silu"], at("silu", b, mt_order(mt) - 1))
                    act.activation(th[:, mt_order(mt) % 2, :], xc[:, mt, :], ACT.Tanh).then_inc(sems["tanh"], 1)

                def exp(a, u):
                    act.wait_ge(sems["row_max"], at("row_max", a, u + 1))
                    act.activation(T[:, u % RING, :], T[:, u % RING, :], ACT.Exp, bias=nmx[:, u % RING:u % RING + 1], scale=-1.0).then_inc(sems["probs"], 1)

                def body(b, a, nxt):
                    for u in range(SLOTS):
                        if a is not None:
                            if u < UNITS:
                                exp(a, u)
                            v = u - LAG
                            if 0 <= v < UNITS and evac_by(v) == "evac_act":
                                g, qt, hh = unit(v)
                                act.wait_ge(sems["turned"], at("turned", a, v + 1))
                                if v % UG in (0, EVAC_DVE[0]):
                                    act.wait_ge(sems["pv"], at("pv", a, g))
                                act.copy(PT[:, hh, :, qt * P:(qt + 1) * P], pt[v % 2][:, :].rearrange("p (k i) -> p k i", i=P)).then_inc(sems["evac_act"], 1)
                            if u >= PV and (u - PV) % UG == 0 and (u - PV) // UG < G:
                                g = (u - PV) // UG
                                act.wait_ge(sems["pv"], at("pv", a, g + 1))
                                act.copy(OTs[:, :], po[:, :]).then_inc(sems["sums_out"], 1)
                            if PROJ <= u < PROJ + C:
                                q = u - PROJ
                                act.wait_ge(sems["heads_turned"], at("heads_turned", a, q + 1))
                                act.wait_ge(sems["projected"], at("projected", a, q - 1))
                                act.copy(OnT[:, q % 2, :, :].rearrange("p k i -> p (k i)"), ps[q % 2][:, 0:KE * P]).then_inc(sems["heads_copied"], 1)
                        for stg in WHEN["act"][u]:
                            mb = nxt if stg[0] in HEAD else b
                            if mb is not None:
                                m(stg, mb)

                def between():
                    act.wait_ge(route_loads, 16 * 3)
                    act.activation(sig_e, sig_e, ACT.Sign).then_inc(step["f_signs"], 1)
                    act.wait_ge(more_consts, MORE)
                    act.wait_ge(setup["scaled"], 1 + KI)

                batches(act, body, between=between)

                def place(k):
                    act.wait_ge(step["f_product"], B // 2 * max(0, k - 1))
                    for j in range(P // SEG):
                        expert = act.value_load(seg_expert[0:1, P // SEG * k + j:P // SEG * k + j + 1], min_val=0, max_val=NT - 1)
                        act.copy(seg_w[k % 2][:, j, :, :], w_f[:, :, bass.ds(expert, 1), :].rearrange("p k o e -> p k (o e)")).then_inc(step["f_placed"], 1)

                act.wait_ge(step["f_rows"], 1)
                act.wait_ge(step["f_w"], 16)
                place(0)
                place(1)
                for m_ in range(PAIRS):
                    if m_ % (B // 2) == 2 and 1 < m_ // (B // 2) + 1 < BLOCKS:
                        place(m_ // (B // 2) + 1)
                    act.wait_ge(step["f_turned"], m_ + 1)
                    act.wait_ge(step["f_product"], max(0, m_ - 1))
                    act.copy(t_f[:, m_ % 2, :], pt[m_ % 2][:, :]).then_inc(step["f_copied"], 1)

            def route(dve):
                done = [0]

                def then(ins):
                    ins.then_inc(step["f_routed"], 1)
                    done[0] += 1
                    dve.wait_ge(step["f_routed"], done[0])

                def view(at_, *shape):
                    n = int(np.prod(shape))
                    ap = tmp[:, at_:at_ + n]
                    return ap.rearrange("p (a b) -> p a b", b=shape[-1]) if len(shape) == 2 else (
                        ap.rearrange("p (a b c) -> p a b c", b=shape[1], c=shape[2]) if len(shape) == 3 else ap)

                def over(ap, shape, axis):
                    letters = {1: "p (o a) -> p o a", 2: "p (a o) -> p a o"}[axis]
                    return ap.rearrange(letters, o=1).broadcast_to(shape)

                oh = view(OH, C, NT)
                sc, key = view(ST, C, NT), view(ST + 32, C, NT)
                best, top = view(ST + 64, C), view(ST + 68, C)
                dve.wait_ge(route_loads, 16 * 3)
                dve.wait_ge(step["f_scores"], 1)
                scores = po[:, 0:C * NT].rearrange("p (c t) -> p c t", t=NT)
                then(dve.tensor_reduce(best, scores, AX.X, ALU.max))
                then(dve.tensor_tensor(sc, scores, over(best, [P, C, NT], 2), ALU.is_equal))
                then(dve.tensor_tensor(key, sc, over(rcol["first"], [P, C, NT], 1), ALU.mult))
                then(dve.tensor_reduce(top, key, AX.X, ALU.max))
                dve.tensor_tensor(oh, key, over(top, [P, C, NT], 2), ALU.is_equal).then_inc(step["f_onehot"], 1)
                dve.wait_ge(step["f_counts"], 1)
                n_at = S // SEG
                many, segs = view(RIGHT + 24, NT, n_at), view(ST + 72, NT)
                count, starts, ends = view(ST + 100, NT), view(ST + 108, NT), view(ST + 116, NT)
                then(dve.tensor_copy(count, po[:, C * NT:(C + 1) * NT]))
                then(dve.tensor_tensor(many, over(count, [P, NT, n_at], 2), over(rcol["seg_at"], [P, NT, n_at], 1), ALU.is_gt))
                then(dve.tensor_reduce(segs, many, AX.X, ALU.add))
                before = view(ST + 130, NT, NT)
                then(dve.tensor_tensor(before, over(segs, [P, NT, NT], 1), rcol["before"].rearrange("p (a b) -> p a b", b=NT), ALU.mult))
                then(dve.tensor_reduce(starts, before, AX.X, ALU.add))
                then(dve.tensor_tensor(ends, starts, segs, ALU.add))
                rank, slot = view(ST + 200, C, NT), view(ST + 232, C)
                then(dve.scalar_tensor_tensor(rank, over(starts, [P, C, NT], 1), float(SEG), po[:, 0:C * NT].rearrange("p (c t) -> p c t", t=NT), ALU.mult, ALU.add))
                then(dve.tensor_tensor(rank, rank, oh, ALU.mult))
                then(dve.tensor_reduce(slot, rank, AX.X, ALU.add))
                then(dve.tensor_scalar(slot, slot, -1.0, None, ALU.add))
                past, block, place = view(ST + 240, C, BLOCKS - 1), view(ST + 262, C), view(ST + 268, C)
                then(dve.tensor_tensor(past, over(slot, [P, C, BLOCKS - 1], 2), over(rcol["block_at"], [P, C, BLOCKS - 1], 1), ALU.is_ge))
                then(dve.tensor_reduce(block, past, AX.X, ALU.add))
                then(dve.scalar_tensor_tensor(place, block, -float(P), slot, ALU.mult, ALU.add))
                left, right = view(LEFT, C, P), view(RIGHT, C, BLOCKS)
                then(dve.tensor_tensor(left, over(rcol["slot"], [P, C, P], 1), over(place, [P, C, P], 2), ALU.is_equal))
                then(dve.tensor_tensor(right, over(rcol["blk"], [P, C, BLOCKS], 1), over(block, [P, C, BLOCKS], 2), ALU.is_equal))
                dve.tensor_tensor(right, right, over(rcol["pos1"], [P, C, BLOCKS], 2), ALU.mult).then_inc(step["f_tables"], 1)
                seg_n, slot_n = view(ST + 280, SEGS, NT), view(ST + 480, BLOCKS, NT)
                seg_f, slot_f = view(ST + 540, SEGS), view(ST + 570, BLOCKS)
                then(dve.tensor_tensor(seg_n, over(ends, [P, SEGS, NT], 1), over(rcol["seg"], [P, SEGS, NT], 2), ALU.is_le))
                then(dve.tensor_reduce(seg_f, seg_n, AX.X, ALU.add))
                then(dve.tensor_scalar(seg_f, seg_f, float(NT - 1), None, ALU.min))
                then(dve.tensor_copy(seg_expert[0:1, :], seg_f[0:1, :]))
                then(dve.tensor_tensor(slot_n, over(ends, [P, BLOCKS, NT], 1), over(rcol["blk_slot"], [P, BLOCKS, NT], 2), ALU.is_le))
                then(dve.tensor_reduce(slot_f, slot_n, AX.X, ALU.add))
                then(dve.tensor_scalar(slot_f, slot_f, float(NT - 1), None, ALU.min))
                then(dve.tensor_copy(expert_of[:, :], slot_f))
                dve.wait_ge(step["f_slots"], 1)
                held, empty = view(ST + 580, BLOCKS), view(ST + 590, BLOCKS)
                then(dve.tensor_scalar(empty, po[:, 0:BLOCKS], 0.0, 1e6, ALU.is_equal, ALU.mult))
                then(dve.scalar_tensor_tensor(held, po[:, 0:BLOCKS], -1.0, empty, ALU.add, ALU.add))
                dve.tensor_copy(row_of[:, :], held).then_inc(step["f_rows"], 1)

            @block.vector
            def _(dve):
                dve.memset(nhalf[:, :], -0.5).then_inc(setup["dve"], 1)
                dve.memset(ones[:, :], 1.0).then_inc(setup["dve"], 1)
                dve.memset(pre[:, :, 0:DC - 1], 0.0).then_inc(setup["dve"], 1)
                dve.wait_ge(consts, CONSTS)
                dve.tensor_scalar(cw[:, :, :], cw[:, :, :], 0.5, None, ALU.mult).then_inc(setup["dve"], 1)
                dve.tensor_scalar(cb[:, :], cb[:, :], 0.5, None, ALU.mult).then_inc(setup["dve"], 1)
                dve.wait_ge(setup["dve"], 5)
                dve.memset(vm[:, :, :, :], 0.0).then_inc(setup["ready"], 1)
                dve.wait_ge(setup["ready"], 3)
                dve.memset(vm[:, :, :, AD:AD + 1], 1.0).then_inc(setup["dve"], 1)

                def between():
                    dve.memset(q_st[:, :, :, :].bitcast(F32), 0.0).then_inc(setup["dve"], 1)
                    dve.memset(k_st[:, :, :, :].bitcast(F32), 0.0).then_inc(setup["dve"], 1)
                    dve.wait_ge(more_consts, MORE)
                    dve.tensor_scalar(bq[:, :], bq[:, :], AD ** -0.5, None, ALU.mult).then_inc(setup["scaled"], 1)
                    for kt in range(KI):
                        dve.tensor_scalar(wout[:, kt, :], wout[:, kt, :], nw[:, kt:kt + 1], 0.5, ALU.mult, ALU.mult).then_inc(setup["scaled"], 1)
                    dve.wait_ge(setup["dve"], 8)
                    route(dve)

                def m(stg, b):
                    k = stg[0]
                    if k == "ln1":
                        dve.wait_ge(sems["x_loaded"], at("x_loaded", b, 16))
                        for c in range(C):
                            dve.bn_stats(st[:, c, :], x_in[:, c, :]).then_inc(sems["stats"], 1)
                        dve.wait_ge(sems["ln_x"], at("ln_x", b, 0))
                        for c in range(C):
                            dve.wait_ge(*alone(dve, sems["stats"], at("stats", b, c + 1)))
                            dve.bn_aggr(mv[:, c, :], st[:, c, :]).then_inc(sems["mean_var"], 1)
                        dve.wait_ge(sems["mean_var"], at("mean_var", b, C))
                        dve.tensor_scalar(ve[:, :, 0:1], mv[:, :, 1:2], EPS, None, ALU.add).then_inc(sems["var_eps"], 1)
                        dve.tensor_scalar(ve[:, :, 1:2], mv[:, :, 1:2], 1.0 + EPS, EPS * EPS, ALU.mult, ALU.add).then_inc(sems["var_eps"], 1)
                    if k == "ln2":
                        dve.wait_ge(sems["rstd"], at("rstd", b, 1))
                        for c in range(C):
                            dve.tensor_scalar(xn[:, c, :], x_in[:, c, :], mv[:, c, 0:1], rs[:, c, 1:2], ALU.subtract, ALU.mult).then_inc(sems["normed"], 1)
                        for c in range(C):
                            dve.tensor_scalar(xr[:, c, :], x_in[:, c, :], mv[:, c, 0:1], rs[:, c, 0:1], ALU.subtract, ALU.mult).then_inc(sems["ln_x"], 1)
                    if k == "dt1":
                        dve.wait_ge(full(("dt",)), full_at(("dt",), b))
                        dve.tensor_tensor(dts[:, 0, :, :], bank(("dt",))[:, 0:C * NH].rearrange("p (c h) -> p c h", h=NH), dtb[:, :, :], ALU.add).then_inc(read(("dt",)), 1)
                        dve.wait_ge(read(("dt",)), read_at(("dt",), b))
                        n = 0

                        def step(ins):
                            ins.then_inc(sems["dt_step"], 1)

                        step(dve.tensor_scalar(dts[:, 3, :, :], dts[:, 0, :, :], 0.0, None, ALU.max))
                        step(dve.scalar_tensor_tensor(dts[:, 1, :, :], dts[:, 0, :, :], -1.0, dts[:, 0, :, :], ALU.mult, ALU.max))
                    if k == "dt2":
                        e, r, y, y2, acc = (dts[:, i, :, :] for i in (2, 4, 5, 6, 7))
                    if stg == ("dt2", 0):
                        dve.wait_ge(sems["dt_exp"], at("dt_exp", b, 1))
                        dve.tensor_scalar(r, e, 2.0, None, ALU.add).then_inc(sems["dt_step"], 1)
                        dve.wait_ge(sems["dt_step"], at("dt_step", b, 3))
                        dve.reciprocal(y, r).then_inc(sems["dt_step"], 1)
                        dve.wait_ge(sems["dt_step"], at("dt_step", b, 4))
                        dve.tensor_tensor(y, y, e, ALU.mult).then_inc(sems["dt_step"], 1)
                    if stg == ("dt2", 1):
                        dve.wait_ge(sems["dt_step"], at("dt_step", b, 5))
                        dve.tensor_tensor(y2, y, y, ALU.mult).then_inc(sems["dt_step"], 1)
                        dve.wait_ge(sems["dt_step"], at("dt_step", b, 6))
                        dve.tensor_scalar(acc, y2, 1.0 / 15, None, ALU.mult).then_inc(sems["dt_step"], 1)
                    if stg in (("dt2", 1), ("dt2", 2)):
                        for i, d in ((0, 13), (1, 11)) if stg[1] == 1 else ((2, 9), (3, 7), (4, 5)):
                            dve.wait_ge(sems["dt_step"], at("dt_step", b, 7 + i))
                            dve.scalar_tensor_tensor(acc, acc, 1.0 / d, y2, ALU.add, ALU.mult).then_inc(sems["dt_step"], 1)
                    if stg == ("dt2", 3):
                        dve.wait_ge(sems["dt_step"], at("dt_step", b, 12))
                        dve.scalar_tensor_tensor(acc, acc, 1.0 / 3, y2, ALU.add, ALU.mult).then_inc(sems["dt_series"], 1)
                        dve.wait_ge(sems["dt_series"], at("dt_series", b, 1))
                        dve.scalar_tensor_tensor(acc, acc, 1.0, y, ALU.add, ALU.mult).then_inc(sems["dt_series"], 1)
                        dve.wait_ge(sems["dt_series"], at("dt_series", b, 2))
                        dve.scalar_tensor_tensor(dt[:, :, :], acc, 2.0, dts[:, 3, :, :], ALU.mult, ALU.add).then_inc(sems["dt_ready"], 1)
                        dve.wait_ge(sems["dt_ready"], at("dt_ready", b, 1))
                        dve.tensor_tensor(dA[:, :, :], dt[:, :, :], nega[:, :].rearrange("p (o h) -> p o h", o=1).broadcast_to([P, C, NH]), ALU.mult).then_inc(sems["dt_ready"], 1)
                    if k == "z":
                        c = stg[1]
                        dve.wait_ge(sems["z_tanh"], at("z_tanh", b, c + 1))
                        dve.scalar_tensor_tensor(zs[:, :], zt[:, c % 2, :], 1.0, bank(stg)[:, :], ALU.add, ALU.mult).then_inc(read(stg), 1)
                    if k == "v":
                        j = stg[1]
                        dve.wait_ge(full(("v", j)), full_at(("v", j), b))
                        if j == 0:
                            dve.wait_ge(sems["va_moved"], at("va_moved", b, 0))
                        for i in range(2):
                            ins = dve.tensor_tensor(vm[:, 2 * j + i, :, 0:AD], bank(("v", j))[:, i * E:(i + 1) * E].rearrange("p (h d) -> p h d", d=AD),
                                                    bvb[:, :].rearrange("p (h d) -> p h d", d=AD), ALU.add)
                            if i == 0:
                                ins.then_inc(sems["v_half"], 1)
                        ins.then_inc(read(("v", j)), 1)
                    if k == "am":
                        c = stg[1]
                        if c == 0:
                            dve.wait_ge(sems["mask_loaded"], at("mask_loaded", b, 16))
                        dve.tensor_scalar(am_m[:, c, :], am_m[:, c, :].bitcast(I32), 0, MASKED, ALU.is_equal, ALU.mult).then_inc(sems["mask_bias"], 1)
                    if k == "gx":
                        c = stg[1]
                        dve.wait_ge(full(("gb", c)), full_at(("gb", c), b))
                        dve.tensor_tensor(Gm[:, :], bank(("gb", c))[:, 0:P], triu[:, :], ALU.mult).then_inc(sems["gram_masked"], 1)
                        dve.tensor_copy(Bt[:, :], bank(("gb", c))[:, P:2 * P]).then_inc(read(("gb", c)), 1)
                    if k == "w":
                        c = stg[1]
                        for j in range(2):
                            dve.wait_ge(read(("seg", j, c)), read_at(("seg", j, c), b))
                        dve.wait_ge(sems["gram_masked"], at("gram_masked", b, c + 1))
                        if c < C - 1:
                            dve.wait_ge(sems["x_decayed"], at("x_decayed", b, c + 1))
                        dve.tensor_tensor(L[:, :, :], L[:, :, :], Gm[:, :].rearrange("p (o i) -> p o i", o=1).broadcast_to([P, NH, P]), ALU.mult).then_inc(sems["weights"], 1)
                    if k in ("inter", "intra", "state"):
                        c = stg[1]
                        v3 = lambda ap: ap.rearrange("p (h d) -> p h d", d=HD)
                    if k == "inter":
                        dve.wait_ge(sems["x_D"], at("x_D", b, c + 1))
                        if c:
                            dve.wait_ge(full(("inter", c)), full_at(("inter", c), b))
                            dve.wait_ge(read(("cum",)), read_at(("cum",), b))
                            dve.tensor_tensor(ti[:, :, :], v3(bank(("inter", c))[:, :]), ecum[:, 0, c, :].rearrange("p (h o) -> p h o", o=1).broadcast_to([P, NH, HD]), ALU.mult).then_inc(read(("inter", c)), 1)
                            dve.wait_ge(read(("inter", c)), read_at(("inter", c), b))
                            dve.tensor_tensor(ti[:, :, :], ti[:, :, :], xD[:, :, :], ALU.add).then_inc(sems["y_inter"], 1)
                    if k == "intra":
                        if c:
                            dve.wait_ge(sems["y_inter"], at("y_inter", b, c))
                        dve.wait_ge(full(("intra", c)), full_at(("intra", c), b))
                        src = ti if c else xD
                        dve.tensor_tensor(ti[:, :, :], v3(bank(("intra", c))[:, :]), src[:, :, :], ALU.add).then_inc(read(("intra", c)), 1)
                    if k == "state":
                        if c < C - 1:
                            dve.wait_ge(full(("state", c)), full_at(("state", c), b))
                            if c:
                                dve.wait_ge(sems["state_decayed"], at("state_decayed", b, c))
                                dve.tensor_tensor(state[:, :, :], v3(bank(("state", c))[:, :]), sdec[:, :, :], ALU.add).then_inc(read(("state", c)), 1)
                            else:
                                dve.tensor_copy(state[:, :, :], v3(bank(("state", c))[:, :])).then_inc(read(("state", c)), 1)
                    if k == "gate":
                        c = stg[1]
                        dve.wait_ge(read(("intra", c)), read_at(("intra", c), b))
                        dve.wait_ge(read(("z", c)), read_at(("z", c), b))
                        dve.tensor_tensor(yg[:, :, :], ti[:, :, :], zs[:, :].rearrange("p (h d) -> p h d", d=HD), ALU.mult).then_inc(sems["y_gated"], 1)
                    if k == "gate2":
                        c = stg[1]
                        dve.wait_ge(sems["sumsq"], at("sumsq", b, c + 1))
                        dve.tensor_scalar(se[:, :], ss[:, :], 0.25 / DI, EPS, ALU.mult, ALU.add).then_inc(sems["meansq"], 1)
                    if k == "x1":
                        c = stg[1]
                        dve.wait_ge(full(("out", c)), full_at(("out", c), b))
                        dve.wait_ge(sems["gate_rstd"], at("gate_rstd", b, c + 1))
                        dve.scalar_tensor_tensor(x1[:, c, :], bank(("out", c))[:, 0:E], rr[:, 0:1], xr[:, c, :], ALU.mult, ALU.add).then_inc(read(("out", c)), 1)
                        dve.wait_ge(read(("out", c)), read_at(("out", c), b))
                        dve.bn_stats(st2[:, :], x1[:, c, :]).then_inc(sems["stats2"], 1)
                        dve.wait_ge(*alone(dve, sems["stats2"], at("stats2", b, c + 1)))
                        dve.bn_aggr(mv2[:, :], st2[:, :]).then_inc(sems["mean_var2"], 1)
                        dve.wait_ge(sems["mean_var2"], at("mean_var2", b, c + 1))
                        dve.tensor_scalar(ve2[:, :], mv2[:, 1:2], EPS, None, ALU.add).then_inc(sems["var_eps2"], 1)
                    if k == "xq":
                        c = stg[1]
                        dve.wait_ge(sems["rstd2"], at("rstd2", b, c + 1))
                        dve.tensor_scalar(xq[:, c, :], x1[:, c, :], mv2[:, 0:1], r2[:, 0:1], ALU.subtract, ALU.mult).then_inc(sems["query_normed"], 1)
                    if k == "silu":
                        silu(b, stg[1])
                    if k == "conv" and stg[1] in ON_DVE:
                        conv(b, stg[1])
                    if k in ("ksplit", "qsplit"):
                        n = k[0]
                        if n == "k":
                            dve.wait_ge(sems["qk_out"], at("qk_out", b, 0))
                        else:
                            dve.wait_ge(sems["qk_out"], at("qk_out", b, 16 * 4))
                        for ct in range(KE):
                            dve.wait_ge(read((n, ct)), read_at((n, ct), b))
                            dve.tensor_copy(kp[:, 0, ct, :], kf[:, ct, :]).then_inc(sems[f"{n}_high"], 1)
                        for ct in range(KE):
                            dve.wait_ge(sems[f"{n}_high"], at(f"{n}_high", b, ct + 1))
                            dve.tensor_tensor(kp[:, 1, ct, :], kf[:, ct, :], kp[:, 0, ct, :].bitcast(F32), ALU.subtract).then_inc(sems[f"{n}_low"], 1)

                def conv(b, mt):
                    src = pre[:, mt_order(mt) % PRE, :]
                    dve.wait_ge(read(("bc", mt)), read_at(("bc", mt), b))
                    dve.tensor_scalar(xc[:, mt, :], src[:, 0:S], cw[:, mt, 0:1], cb[:, mt:mt + 1], ALU.mult, ALU.add).then_inc(sems["conv_dve"], 1)
                    for j in range(1, DC):
                        dve.wait_ge(sems[conv_by(mt)], at(conv_by(mt), b, taps_at(mt, j)))
                        dve.scalar_tensor_tensor(xc[:, mt, :], src[:, j:j + S], cw[:, mt, j:j + 1], xc[:, mt, :], ALU.mult, ALU.add).then_inc(sems["conv_dve"], 1)

                def silu(b, mt):
                    i = mt_order(mt)
                    dve.wait_ge(sems["tanh"], at("tanh", b, i + 1))
                    dve.scalar_tensor_tensor(xc[:, mt, :], th[:, i % 2, :], 1.0, xc[:, mt, :], ALU.add, ALU.mult).then_inc(sems["silu"], 1)

                def take_max(a, u):
                    g, qt, hh = unit(u)
                    if u == 0:
                        dve.wait_ge(sems["bias_moved01"], at("bias_moved01", a, 16))
                    if u == 2:
                        dve.wait_ge(sems["bias_moved23"], at("bias_moved23", a, 16))
                    dve.wait_ge(*alone(dve, sems["score"], at("score", a, u + 1)))
                    dve.tensor_tensor_reduce(T[:, u % RING, :], ps[u % 2][:, :], am[:, qt, :], -1.0, 3e38, ALU.add, ALU.min, nmx[:, u % RING:u % RING + 1]).then_inc(sems["row_max"], 1)

                def body(b, a, nxt):
                    for u in range(SLOTS):
                        if a is not None:
                            if u < UNITS:
                                take_max(a, u)
                            v = u - LAG
                            if 0 <= v < UNITS and evac_by(v) == "evac_dve":
                                g, qt, hh = unit(v)
                                dve.wait_ge(sems["turned"], at("turned", a, v + 1))
                                if v % UG in (0, EVAC_DVE[0]):
                                    dve.wait_ge(sems["pv"], at("pv", a, g))
                                dve.tensor_copy(PT[:, hh, :, qt * P:(qt + 1) * P], pt[v % 2][:, :].rearrange("p (k i) -> p k i", i=P)).then_inc(sems["evac_dve"], 1)
                            if u >= PV + 2 and (u - PV - 2) % UG == 0 and (u - PV - 2) // UG < G:
                                g = (u - PV - 2) // UG
                                dve.wait_ge(sems["sums_turned"], at("sums_turned", a, g + 1))
                                po4 = po[:, :].rearrange("p (q h v) -> p q h v", q=C, h=HG)
                                dve.reciprocal(rden[:, :, :], po4[:, :, :, AD]).then_inc(sems["recip"], 1)
                                dve.wait_ge(sems["recip"], at("recip", a, g + 1))
                                for q in range(C):
                                    ins = dve.tensor_tensor(On[:, q, g * HG:(g + 1) * HG, :], po4[:, q, :, 0:AD],
                                                            rden[:, q, :].rearrange("p (h o) -> p h o", o=1).broadcast_to([P, HG, AD]), ALU.mult)
                                ins.then_inc(sems["heads_normed"], 1)
                            if PROJ + 1 <= u < PROJ + 1 + C:
                                q = u - PROJ - 1
                                dve.wait_ge(sems["projected"], at("projected", a, q + 1))
                                if q == 0:
                                    dve.wait_ge(sems["x1a_moved"], at("x1a_moved", a, 16))
                                dve.tensor_tensor(x1a[:, q, :], pt[q % 2][:, 0:E], x1a[:, q, :], ALU.add).then_inc(sems["x2_rows"], 1)
                        for stg in WHEN["dve"][u]:
                            mb = nxt if stg[0] in HEAD else b
                            if mb is not None:
                                m(stg, mb)

                batches(dve, body, between=between)

                def stats(k, rows):
                    if rows[0] == 0:
                        dve.wait_ge(f_in[k % BUFS], 16 * (k // BUFS + 1))
                        dve.wait_ge(step["f_normed"], B * max(0, k - 1))
                    for j in rows:
                        dve.bn_stats(st_f[:, k % 2, 6 * j:6 * (j + 1)], x_f[k % BUFS][:, j * E:(j + 1) * E]).then_inc(step["f_stats"], 1)
                    for j in rows:
                        dve.wait_ge(step["f_stats"], B * k + j + 1)
                        dve.bn_aggr(mv_f[:, k % 2, 2 * j:2 * j + 2], st_f[:, k % 2, 6 * j:6 * (j + 1)]).then_inc(step["f_mean_var"], 1)
                    if rows[-1] == B - 1:
                        dve.wait_ge(step["f_mean_var"], B * (k + 1))
                        dve.tensor_scalar(ve_f[:, k % 2, :].rearrange("p (j o) -> p j o", o=1), mv_f[:, k % 2, :].rearrange("p (j o) -> p j o", o=2)[:, :, 1:2], EPS, None, ALU.add).then_inc(step["f_var_eps"], 1)

                stats(0, range(B))
                for m_ in range(PAIRS + 2):
                    k, n = m_ // (B // 2), m_ % (B // 2)
                    if m_ < PAIRS:
                        dve.wait_ge(step["f_rstd"], k + 1)
                        dve.wait_ge(step["f_turned"], max(0, m_ - 1))
                        for j in (2 * n, 2 * n + 1):
                            dve.tensor_scalar(n_f[:, m_ % 2, j % 2 * E:(j % 2 + 1) * E], x_f[k % BUFS][:, j * E:(j + 1) * E], mv_f[:, k % 2, 2 * j:2 * j + 1], r_f[:, k % 2, j:j + 1],
                                              ALU.subtract, ALU.mult).then_inc(step["f_normed"], 1)
                        if k + 1 < BLOCKS:
                            stats(k + 1, (2 * n, 2 * n + 1))
                    if m_ >= 2:
                        w = m_ - 2
                        dve.wait_ge(step["f_biased"], w + 1)
                        dve.wait_ge(step["f_product"], w + 1)
                        two = x_f[w // (B // 2) % BUFS][:, w % (B // 2) * 2 * E:(w % (B // 2) + 1) * 2 * E]
                        dve.tensor_tensor(two, ps[w % 2][:, :], two, ALU.add).then_inc(step["f_sum"], 1)

            @block.gpsimd
            def _(pool):
                pool.wait_ge(consts, CONSTS)
                pool.memset(state[:, :, :], 0.0).then_inc(setup["ready"], 1)
                pool.wait_ge(setup["ready"], 3)

                def conv(b, mt):
                    src, n = pre[:, mt_order(mt) % PRE, :], ON_POOL.index(mt)
                    pool.wait_ge(*alone(pool, read(("bc", mt)), read_at(("bc", mt), b)))
                    pool.tensor_scalar(xc[:, mt, :], src[:, 0:S], cw[:, mt, 0:1], cb[:, mt:mt + 1], ALU.mult, ALU.add).then_inc(sems["conv_pool"], 1)
                    for j in range(1, DC):
                        if j > 1 or n:
                            pool.wait_ge(*alone(pool, sems[conv_by(ON_POOL[n if j > 1 else n - 1])], at(conv_by(ON_POOL[n if j > 1 else n - 1]), b, taps_at(ON_POOL[n if j > 1 else n - 1], j if j > 1 else DC))))
                        pool.tensor_scalar(tap[:, :, :].rearrange("p k i -> p (k i)"), src[:, j:j + S], cw[:, mt, j:j + 1], 0.0, ALU.mult, ALU.add).then_inc(sems["tap_product"], 1)
                        pool.wait_ge(sems[conv_by(mt)], at(conv_by(mt), b, taps_at(mt, j)))
                        pool.wait_ge(sems["tap_product"], at("tap_product", b, (DC - 1) * n + j))
                        pool.tensor_tensor(xc[:, mt, :], xc[:, mt, :], tap[:, :, :].rearrange("p k i -> p (k i)"), ALU.add).then_inc(sems["conv_pool"], 1)

                def m(stg, b):
                    k = stg[0]
                    if k == "ln1":
                        pool.wait_ge(sems["var_eps"], at("var_eps", b, 2))
                        pool.tensor_tensor(rs[:, :, :].rearrange("p c k -> p (c k)"), ve[:, :, :].rearrange("p c k -> p (c k)"), nhalf[:, 0:2 * C], ALU.pow).then_inc(sems["rstd"], 1)
                    if k == "ln2":
                        pool.wait_ge(sems["ln_x"], at("ln_x", b, C))
                        pool.tensor_tensor(xr[:, :, :], x_in[:, :, :], xr[:, :, :], ALU.add).then_inc(sems["residual"], 1)
                    if k == "conv" and stg[1] in ON_POOL:
                        conv(b, stg[1])
                    if stg == ("am", C - 1):
                        pool.wait_ge(*alone(pool, sems["mask_bias"], at("mask_bias", b, C)))
                        pool.dma_start(am_m[:, :, :], t["adj"].rearrange("(c p) s -> p c s", p=P), accum_op=ALU.add).then_inc(sems["score_bias"], 16)
                    if k == "dmask":
                        c = stg[1]
                        pool.wait_ge(sems["dt_ready"], at("dt_ready", b, 2))
                        pool.wait_ge(full(("intra", c - 1 if c else C - 1)), full_at(("intra", c - 1 if c else C - 1), b if c else b - 1))
                        pool.tensor_tensor(dmask[:, :, :], triu[:, :].rearrange("p (o i) -> p o i", o=1).broadcast_to([P, NH, P]),
                                           dA[:, c, :].rearrange("p (h o) -> p h o", o=1).broadcast_to([P, NH, P]), ALU.mult).then_inc(sems["decay_mask"], 1)
                    if k == "gx":
                        c = stg[1]
                        pool.wait_ge(read(("xt", c)), read_at(("xt", c), b))
                        if c:
                            pool.wait_ge(full(("intra", c - 1)), full_at(("intra", c - 1), b))
                            pool.wait_ge(sems["y_gated"], at("y_gated", b, c))
                        pool.tensor_tensor(xdt[:, :, :], xt[:, :, :], dt[:, c, :].rearrange("p (h o) -> p h o", o=1).broadcast_to([P, NH, HD]), ALU.mult).then_inc(sems["x_dt"], 1)
                        if c < C - 1:
                            if c:
                                pool.wait_ge(full(("state", c - 1)), full_at(("state", c - 1), b))
                            pool.wait_ge(sems["x_dt"], at("x_dt", b, c + 1))
                            for j in range(2):
                                pool.wait_ge(read(("seg", j, c)), read_at(("seg", j, c), b))
                            pool.tensor_tensor(xw[:, :, :], xdt[:, :, :], L[:, :, P - 1:P].broadcast_to([P, NH, HD]), ALU.mult).then_inc(sems["x_decayed"], 1)
                        pool.wait_ge(sems["x_dt"], at("x_dt", b, c + 1))
                        pool.tensor_tensor(xD[:, :, :], xt[:, :, :], dsk[:, :].rearrange("p (h o) -> p h o", o=1).broadcast_to([P, NH, HD]), ALU.mult).then_inc(sems["x_D"], 1)
                    if k == "sdec":
                        c = stg[1]
                        if 0 < c < C - 1:
                            pool.wait_ge(full(("inter", c)), full_at(("inter", c), b))
                            pool.wait_ge(read(("state", c - 1)), read_at(("state", c - 1), b))
                            if read(("cum",)) is not read(("state", c - 1)):
                                pool.wait_ge(read(("cum",)), read_at(("cum",), b))
                            pool.tensor_tensor(sdec[:, :, :], state[:, :, :], ecum[:, 1, c, :].rearrange("p (h o) -> p h o", o=1).broadcast_to([P, NH, HD]), ALU.mult).then_inc(sems["state_decayed"], 1)
                    if k == "gate2":
                        c = stg[1]
                        pool.wait_ge(sems["meansq"], at("meansq", b, c + 1))
                        pool.tensor_tensor(rr[:, :], se[:, :], nhalf[:, 0:1], ALU.pow).then_inc(sems["gate_rstd"], 1)
                    if k == "x1":
                        c = stg[1]
                        pool.wait_ge(sems["var_eps2"], at("var_eps2", b, c + 1))
                        pool.tensor_tensor(r2[:, :], ve2[:, :], nhalf[:, 0:1], ALU.pow).then_inc(sems["rstd2"], 1)
                    if k == "xq":
                        c = stg[1]
                        pool.wait_ge(sems["query_normed"], at("query_normed", b, c + 1))
                        pool.tensor_tensor(x1b[:, c, :], x1[:, c, :], bob[:, :], ALU.add).then_inc(sems["x1_bias"], 1)

                def body(b, a, nxt):
                    for u in range(SLOTS):
                        for stg in WHEN["pool"][u]:
                            mb = nxt if stg[0] in HEAD else b
                            if mb is not None:
                                m(stg, mb)

                def between():
                    pool.wait_ge(more_consts, MORE)

                batches(pool, body, between=between)

                def gather(k):
                    pool.indirect_dma_start(x_f[k % BUFS], None, x2_d, bass.IndirectOffsetOnAxis(row_of[:, k:k + 1].bitcast(U32), 0),
                                            bounds_check=S - 1, oob_is_err=False).then_inc(f_in[k % BUFS], 16)

                pool.wait_ge(step["f_rows"], 1)
                pool.wait_ge(sems["va_moved"], at("va_moved", B, 0))
                for k in range(BLOCKS):
                    pool.indirect_dma_start(b_f[:, k, :], None, t["b_f"], bass.IndirectOffsetOnAxis(expert_of[:, k:k + 1].bitcast(U32), 0),
                                            bounds_check=NT - 1, oob_is_err=False).then_inc(step["f_b"], 16)
                pool.wait_ge(sems["x2_out0"], at("x2_out0", B, 0))
                pool.wait_ge(sems["x2_out1"], at("x2_out1", B, 0))
                for k in range(BUFS):
                    gather(k)
                pool.wait_ge(step["f_b"], 16 * BLOCKS)

                def rstd(k):
                    pool.wait_ge(step["f_var_eps"], k + 1)
                    pool.tensor_tensor(r_f[:, k % 2, :], ve_f[:, k % 2, :], nhalf[:, 0:B], ALU.pow).then_inc(step["f_rstd"], 1)

                def scatter(k):
                    pool.wait_ge(step["f_sum"], B // 2 * (k + 1))
                    pool.indirect_dma_start(t["out"], bass.IndirectOffsetOnAxis(row_of[:, k:k + 1].bitcast(U32), 0), x_f[k % BUFS], None,
                                            bounds_check=S - 1, oob_is_err=False).then_inc(f_out[k % BUFS], 16)

                rstd(0)
                for m_ in range(PAIRS):
                    k, n = m_ // (B // 2), m_ % (B // 2)
                    pool.wait_ge(step["f_normed"], 2 * (m_ + 1))
                    rows = x_f[k % BUFS][:, 2 * n * E:2 * (n + 1) * E].rearrange("p (b e) -> p b e", e=E)
                    pool.tensor_tensor(rows, rows, b_f[:, k, :].rearrange("p (o e) -> p o e", o=1).broadcast_to([P, 2, E]), ALU.add).then_inc(step["f_biased"], 1)
                    if n == 1 and k:
                        scatter(k - 1)
                    if n == 3:
                        if k + 1 < BLOCKS:
                            rstd(k + 1)
                        if k and k - 1 + BUFS < BLOCKS:
                            pool.wait_ge(f_out[(k - 1) % BUFS], 16 * ((k - 1) // BUFS + 1))
                            gather(k - 1 + BUFS)
                scatter(BLOCKS - 1)


def _positions():
    div = np.exp(np.arange(0, PD, 2, dtype=np.float32) * np.float32(-np.log(10000.0) / PD))
    ang = np.arange(S, dtype=np.float32)[:, None] * div
    pe = np.zeros((S, PD), np.float32)
    pe[:, 0::2], pe[:, 1::2] = np.sin(ang), np.cos(ang)
    return pe


def _route_table():
    p, t_ = np.arange(P), np.arange(NT)
    rows = dict(slot=np.arange(P), first=NT - t_, seg_at=SEG * np.arange(S // SEG), seg=np.arange(SEGS), before=(t_[None, :] < t_[:, None]).reshape(-1),
                block_at=P * np.arange(1, BLOCKS), blk=np.arange(BLOCKS), blk_slot=(P * np.arange(BLOCKS)[None, :] + p[:, None]) // SEG,
                pos1=P * np.arange(C)[None, :] + p[:, None] + 1)
    return np.concatenate([np.broadcast_to(rows[k], (P, w)) for k, w in RT.items()], 1).astype(np.float32)


def _arrays(x, ctx_1024, mask_Bx1xSxS2_ik1, **w):
    def lay(a):
        return np.ascontiguousarray(np.asarray(a))

    n = {k[3:]: np.asarray(v) for k, v in w.items()}
    ip = n["attn_in_proj_w"]
    row, col = np.arange(P)[:, None], np.arange(P)[None, :]
    return dict(
        x=lay(np.asarray(x).reshape(B * S, E)),
        ctxT=lay(np.asarray(ctx_1024).transpose(0, 2, 1).reshape(B * E, S)),
        mask=lay(np.asarray(mask_Bx1xSxS2_ik1).reshape(B * S, S)),
        wz=lay(ip[:DI].T), wxbc=lay(ip[DI:DI + CT * P].T), wdt=lay(ip[DI + CT * P:].T),
        conv_w=lay(n["attn_conv_w"]), conv_b=lay(n["attn_conv_b"]), dt_bias=lay(n["attn_dt_bias"]),
        A_log=lay(n["attn_A_log"]), D=lay(n["attn_D"]), norm_w=lay(n["attn_norm_w"]),
        ln_w=lay(n["attn_ln_w"]), ln_b=lay(n["attn_ln_b"]), wout=lay(n["attn_out_proj_w"].T),
        adj=lay(n["xattn_adj"]), wq=lay(n["xattn_Wq"].T), wk=lay(n["xattn_Wk"].T), wv=lay(n["xattn_Wv"].T),
        wo=lay(n["xattn_Wo"].T), bq=lay(n["xattn_bq"]), bk=lay(n["xattn_bk"]), bv=lay(n["xattn_bv"]), bo=lay(n["xattn_bo"]),
        w_f=lay(n["ffn_W"].transpose(2, 0, 1)), b_f=lay(n["ffn_b"]), sigs=lay(n["ffn_tile_sigs"].T), pe=lay(_positions().T), rt=_route_table(),
        ident=np.eye(P, dtype=np.float32), triu=(row <= col).astype(np.float32), stril=(row > col).astype(np.float32),
    )


def kernel(**inputs):
    import concourse.bacc as bacc
    from concourse.bass_utils import run_bass_kernel_spmd

    nc = bacc.Bacc("TRN2", target_bir_lowering=False, num_devices=1)
    arrays = {f"in_{k}": v for k, v in _arrays(**inputs).items()}
    t = {k[3:]: nc.dram_tensor(k, v.shape, mybir.dt.from_np(v.dtype), kind="ExternalInput").ap() for k, v in arrays.items()}
    t["out"] = nc.dram_tensor("out", (S, ROW), F32, kind="ExternalOutput").ap()
    build(nc, t)
    r = run_bass_kernel_spmd(nc, [arrays], core_ids=[0])
    return np.ascontiguousarray(r.results[0]["out"].reshape(S, B, E).transpose(1, 0, 2))
```
